# Optimizing a Trainium2 kernel written in Bass

```python
import numpy as np
import jax
import jax.numpy as jnp

def _softmax(x, axis=-1):
    return jax.nn.softmax(x, axis=axis)

def _gelu(x):
    return jax.nn.gelu(x, approximate=True)

def _silu(x):
    return jax.nn.silu(x)

def _sigmoid(x):
    return jax.nn.sigmoid(x)

def _layernorm(x, axis=-1, eps=1e-05):
    m = jnp.mean(x, axis=axis, keepdims=True)
    v = jnp.var(x, axis=axis, keepdims=True)
    return (x - m) / jnp.sqrt(v + eps)

def _scatter_add(tgt, idx, src, axis=0):
    return tgt.at[idx].add(src)

def _segment_sum(src, seg, n):
    return jax.ops.segment_sum(src, seg, n)
kernel_name = 'mk_prb_d2_jaxref_r4_fd5a7d'

def setup_inputs(seed: int=0):
    np.random.seed(seed)
    _w = jnp.asarray

    def _L0_attn_setup():
        import jax, jax.numpy as jnp
        import numpy as np
        B, T, D = (2, 512, 256)
        H = 16
        HD = D // H
        DL = 128
        NR = 64
        EPS = 1.1920929e-07

        def _rms_norm(x, w):
            ms = jnp.mean(jnp.square(x), axis=-1, keepdims=True)
            return x * jax.lax.rsqrt(ms + EPS) * w
        key = jax.random.key(seed)
        ks = jax.random.split(key, 10)
        s = 0.02
        return {'x': jax.random.normal(ks[0], (B, T, D), dtype=jnp.float32), 'W_DQ': jax.random.normal(ks[1], (DL, HD), dtype=jnp.float32) * s, 'W_UQ': jax.random.normal(ks[2], (HD, DL), dtype=jnp.float32) * s, 'W_DKV': jax.random.normal(ks[3], (2 * DL, HD), dtype=jnp.float32) * s, 'W_UKV': jax.random.normal(ks[4], (2 * HD, 2 * DL), dtype=jnp.float32) * s, 'W_QR': jax.random.normal(ks[5], (NR, HD), dtype=jnp.float32) * s, 'W_KR': jax.random.normal(ks[6], (NR, HD), dtype=jnp.float32) * s, 'W_O': jax.random.normal(ks[7], (HD, HD), dtype=jnp.float32) * s, 'q_norm_w': jnp.ones((HD,), dtype=jnp.float32), 'k_norm_w': jnp.ones((HD,), dtype=jnp.float32)}
    _L0_attn_in = _L0_attn_setup()

    def _L0_ffn_setup():
        import jax, jax.numpy as jnp
        import numpy as np
        SWIGLU_ALPHA = 1.702
        SWIGLU_LIMIT = 7.0
        TOP_K = 4
        key = jax.random.key(seed)
        k = jax.random.split(key, 5)
        B, S, D, E, I = (2, 256, 256, 8, 512)
        return {'hidden_states': jax.random.normal(k[0], (B, S, D), dtype=jnp.float32), 'router_weight': jax.random.normal(k[1], (E, D), dtype=jnp.float32) * 0.02, 'router_bias': jnp.zeros((E,), dtype=jnp.float32), 'gate_up_proj': jax.random.normal(k[2], (E, 2 * I, D), dtype=jnp.float32) * 0.02, 'gate_up_proj_bias': jnp.zeros((E, 2 * I), dtype=jnp.float32), 'down_proj': jax.random.normal(k[3], (E, D, I), dtype=jnp.float32) * 0.02, 'down_proj_bias': jnp.zeros((E, D), dtype=jnp.float32)}
    _L0_ffn_in = _L0_ffn_setup()

    def _L1_attn_setup():
        import jax, jax.numpy as jnp
        import numpy as np
        B, L, D, H = (2, 512, 256, 16)
        HD = D // H
        NEG = -1000000000.0

        def sparsemax(z):
            n = z.shape[-1]
            z_sorted = jnp.flip(jnp.sort(z, axis=-1), axis=-1)
            cssv = jnp.cumsum(z_sorted, axis=-1)
            r = jnp.arange(1, n + 1, dtype=z.dtype)
            support = 1.0 + r * z_sorted > cssv
            k = jnp.sum(support, axis=-1, keepdims=True)
            cssv_k = jnp.take_along_axis(cssv, k - 1, axis=-1)
            tau = (cssv_k - 1.0) / k.astype(z.dtype)
            return jnp.maximum(z - tau, 0.0)
        key = jax.random.key(seed)
        ks = jax.random.split(key, 5)
        s = 1.0 / np.sqrt(D)
        return {'x': jax.random.normal(ks[0], (B, L, D), dtype=jnp.float32), 'Wq': jax.random.normal(ks[1], (D, D), dtype=jnp.float32) * s, 'Wk': jax.random.normal(ks[2], (D, D), dtype=jnp.float32) * s, 'Wv': jax.random.normal(ks[3], (D, D), dtype=jnp.float32) * s, 'Wo': jax.random.normal(ks[4], (D, D), dtype=jnp.float32) * s}
    _L1_attn_in = _L1_attn_setup()

    def _L1_ffn_setup():
        import jax, jax.numpy as jnp
        import numpy as np
        B, S, D = (2, 512, 256)
        H, HKV = (16, 4)
        HD = D // H
        F, E, K = (512, 8, 2)
        THETA = 10000.0
        EPS = 1e-05

        def _rmsnorm(x, w):
            return x * jax.lax.rsqrt(jnp.mean(x * x, axis=-1, keepdims=True) + EPS) * w

        def _rope_cos_sin(seq_len, head_dim, theta):
            inv_freq = 1.0 / theta ** (jnp.arange(0, head_dim, 2, dtype=jnp.float32) / head_dim)
            freqs = jnp.arange(seq_len, dtype=jnp.float32)[:, None] * inv_freq
            return (jnp.cos(freqs), jnp.sin(freqs))

        def _apply_rope(x, cos, sin):
            x1, x2 = jnp.split(x, 2, axis=-1)
            c = cos[None, :, None, :]
            s = sin[None, :, None, :]
            return jnp.concatenate([x1 * c - x2 * s, x2 * c + x1 * s], axis=-1)
        key = jax.random.key(seed)
        ks = jax.random.split(key, 12)
        s = 0.02
        return {'hidden_states': jax.random.normal(ks[0], (B, S, D), jnp.float32), 'ln1_w': 1.0 + 0.1 * jax.random.normal(ks[1], (D,), jnp.float32), 'ln2_w': 1.0 + 0.1 * jax.random.normal(ks[2], (D,), jnp.float32), 'Wq': s * jax.random.normal(ks[3], (D, H * HD), jnp.float32), 'Wk': s * jax.random.normal(ks[4], (D, HKV * HD), jnp.float32), 'Wv': s * jax.random.normal(ks[5], (D, HKV * HD), jnp.float32), 'Wo': s * jax.random.normal(ks[6], (H * HD, D), jnp.float32), 'Wr': s * jax.random.normal(ks[7], (D, E), jnp.float32), 'Wg': s * jax.random.normal(ks[8], (E, D, F), jnp.float32), 'Wu': s * jax.random.normal(ks[9], (E, D, F), jnp.float32), 'Wd': s * jax.random.normal(ks[10], (E, F, D), jnp.float32)}
    _L1_ffn_in = _L1_ffn_setup()
    _d = {'L0_attn_x': _L0_attn_in['x'], 'L0_attn_W_DQ': _L0_attn_in['W_DQ'], 'L0_attn_W_UQ': _L0_attn_in['W_UQ'], 'L0_attn_W_DKV': _L0_attn_in['W_DKV'], 'L0_attn_W_UKV': _L0_attn_in['W_UKV'], 'L0_attn_W_QR': _L0_attn_in['W_QR'], 'L0_attn_W_KR': _L0_attn_in['W_KR'], 'L0_attn_W_O': _L0_attn_in['W_O'], 'L0_attn_q_norm_w': _L0_attn_in['q_norm_w'], 'L0_attn_k_norm_w': _L0_attn_in['k_norm_w'], 'L0_ffn_router_weight': _L0_ffn_in['router_weight'], 'L0_ffn_router_bias': _L0_ffn_in['router_bias'], 'L0_ffn_gate_up_proj': _L0_ffn_in['gate_up_proj'], 'L0_ffn_gate_up_proj_bias': _L0_ffn_in['gate_up_proj_bias'], 'L0_ffn_down_proj': _L0_ffn_in['down_proj'], 'L0_ffn_down_proj_bias': _L0_ffn_in['down_proj_bias'], 'L1_attn_Wq': _L1_attn_in['Wq'], 'L1_attn_Wk': _L1_attn_in['Wk'], 'L1_attn_Wv': _L1_attn_in['Wv'], 'L1_attn_Wo': _L1_attn_in['Wo'], 'L1_ffn_ln1_w': _L1_ffn_in['ln1_w'], 'L1_ffn_ln2_w': _L1_ffn_in['ln2_w'], 'L1_ffn_Wq': _L1_ffn_in['Wq'], 'L1_ffn_Wk': _L1_ffn_in['Wk'], 'L1_ffn_Wv': _L1_ffn_in['Wv'], 'L1_ffn_Wo': _L1_ffn_in['Wo'], 'L1_ffn_Wr': _L1_ffn_in['Wr'], 'L1_ffn_Wg': _L1_ffn_in['Wg'], 'L1_ffn_Wu': _L1_ffn_in['Wu'], 'L1_ffn_Wd': _L1_ffn_in['Wd']}
    _x0 = _d['L0_attn_x']
    _d['L0_attn_x'] = jax.random.normal(jax.random.fold_in(jax.random.key(seed), 1), (8, 512, 256), dtype=_x0.dtype)
    del _x0
    return _d

def reference(L0_attn_x, L0_attn_W_DQ, L0_attn_W_UQ, L0_attn_W_DKV, L0_attn_W_UKV, L0_attn_W_QR, L0_attn_W_KR, L0_attn_W_O, L0_attn_q_norm_w, L0_attn_k_norm_w, L0_ffn_router_weight, L0_ffn_router_bias, L0_ffn_gate_up_proj, L0_ffn_gate_up_proj_bias, L0_ffn_down_proj, L0_ffn_down_proj_bias, L1_attn_Wq, L1_attn_Wk, L1_attn_Wv, L1_attn_Wo, L1_ffn_ln1_w, L1_ffn_ln2_w, L1_ffn_Wq, L1_ffn_Wk, L1_ffn_Wv, L1_ffn_Wo, L1_ffn_Wr, L1_ffn_Wg, L1_ffn_Wu, L1_ffn_Wd):

    def _L0_attn_ref(x, W_DQ, W_UQ, W_DKV, W_UKV, W_QR, W_KR, W_O, q_norm_w, k_norm_w):
        import jax, jax.numpy as jnp
        import numpy as np
        B, T, D = (2, 512, 256)
        H = 16
        HD = D // H
        DL = 128
        NR = 64
        EPS = 1.1920929e-07

        def _rms_norm(x, w):
            ms = jnp.mean(jnp.square(x), axis=-1, keepdims=True)
            return x * jax.lax.rsqrt(ms + EPS) * w
        b, t, d = x.shape
        scale = HD ** (-0.5)
        xh = x.reshape(b, t, H, HD).transpose(0, 2, 1, 3)
        c_q = jnp.einsum('bhtd,ld->bhtl', xh, W_DQ)
        q_c = jnp.einsum('bhtl,dl->bhtd', c_q, W_UQ)
        q_c_norm = _rms_norm(q_c, q_norm_w)
        q_r = jnp.einsum('bhtd,rd->bhtr', q_c_norm, W_QR)
        q = jnp.concatenate([q_c_norm, q_r], axis=-1)
        c_kv = jnp.einsum('bhtd,ld->bhtl', xh, W_DKV)
        kv = jnp.einsum('bhtl,dl->bhtd', c_kv, W_UKV)
        k_c, v_c = (kv[..., :HD], kv[..., HD:])
        k_c_norm = _rms_norm(k_c, k_norm_w)
        k_r = jnp.einsum('bhtd,rd->bhtr', xh, W_KR)
        k = jnp.concatenate([k_c_norm, k_r], axis=-1)
        scores = jnp.einsum('bhqd,bhkd->bhqk', q, k) * scale
        causal = jnp.triu(jnp.full((t, t), -jnp.inf, dtype=scores.dtype), k=1)
        attn = jax.nn.softmax(scores + causal, axis=-1)
        ctx = jnp.einsum('bhqk,bhkd->bhqd', attn, v_c)
        out = jnp.einsum('bhtd,od->bhto', ctx, W_O)
        return out.transpose(0, 2, 1, 3).reshape(b, t, d)

    def _L0_ffn_ref(hidden_states, router_weight, router_bias, gate_up_proj, gate_up_proj_bias, down_proj, down_proj_bias):
        import jax, jax.numpy as jnp
        import numpy as np
        SWIGLU_ALPHA = 1.702
        SWIGLU_LIMIT = 7.0
        TOP_K = 4
        B, S, D = hidden_states.shape
        E = router_weight.shape[0]
        x = hidden_states.reshape(-1, D)
        N = x.shape[0]
        logits = x @ router_weight.T + router_bias
        topk_logits, topk_idx = jax.lax.top_k(logits, TOP_K)
        topk_w = jax.nn.softmax(topk_logits.astype(jnp.float32), axis=-1)
        combine = jnp.zeros((N, E), dtype=jnp.float32)
        combine = combine.at[jnp.arange(N)[:, None], topk_idx].set(topk_w)
        gate_up = jnp.einsum('nd,ejd->nej', x, gate_up_proj) + gate_up_proj_bias
        gate, up = jnp.split(gate_up, 2, axis=-1)
        gate = jnp.minimum(gate, SWIGLU_LIMIT)
        up = jnp.clip(up, -SWIGLU_LIMIT, SWIGLU_LIMIT)
        act = (up + 1.0) * gate * jax.nn.sigmoid(SWIGLU_ALPHA * gate)
        out = jnp.einsum('nei,edi->ned', act, down_proj) + down_proj_bias
        y = jnp.einsum('ned,ne->nd', out, combine.astype(out.dtype))
        return y.reshape(B, S, D)

    def _L1_attn_ref(x, Wq, Wk, Wv, Wo):
        import jax, jax.numpy as jnp
        import numpy as np
        B, L, D, H = (2, 512, 256, 16)
        HD = D // H
        NEG = -1000000000.0

        def sparsemax(z):
            n = z.shape[-1]
            z_sorted = jnp.flip(jnp.sort(z, axis=-1), axis=-1)
            cssv = jnp.cumsum(z_sorted, axis=-1)
            r = jnp.arange(1, n + 1, dtype=z.dtype)
            support = 1.0 + r * z_sorted > cssv
            k = jnp.sum(support, axis=-1, keepdims=True)
            cssv_k = jnp.take_along_axis(cssv, k - 1, axis=-1)
            tau = (cssv_k - 1.0) / k.astype(z.dtype)
            return jnp.maximum(z - tau, 0.0)
        b, l, d = x.shape

        def proj(W):
            return jnp.einsum('bld,ed->ble', x, W).reshape(b, l, H, HD).transpose(0, 2, 1, 3)
        q, k, v = (proj(Wq), proj(Wk), proj(Wv))
        scores = jnp.einsum('bhqd,bhkd->bhqk', q, k) / np.sqrt(HD)
        causal = jnp.tril(jnp.ones((l, l), dtype=bool))
        scores = jnp.where(causal, scores, NEG)
        attn = sparsemax(scores)
        out = jnp.einsum('bhqk,bhkd->bhqd', attn, v)
        out = out.transpose(0, 2, 1, 3).reshape(b, l, d)
        return jnp.einsum('bld,ed->ble', out, Wo)

    def _L1_ffn_ref(hidden_states, ln1_w, ln2_w, Wq, Wk, Wv, Wo, Wr, Wg, Wu, Wd):
        import jax, jax.numpy as jnp
        import numpy as np
        B, S, D = (2, 512, 256)
        H, HKV = (16, 4)
        HD = D // H
        F, E, K = (512, 8, 2)
        THETA = 10000.0
        EPS = 1e-05

        def _rmsnorm(x, w):
            return x * jax.lax.rsqrt(jnp.mean(x * x, axis=-1, keepdims=True) + EPS) * w

        def _rope_cos_sin(seq_len, head_dim, theta):
            inv_freq = 1.0 / theta ** (jnp.arange(0, head_dim, 2, dtype=jnp.float32) / head_dim)
            freqs = jnp.arange(seq_len, dtype=jnp.float32)[:, None] * inv_freq
            return (jnp.cos(freqs), jnp.sin(freqs))

        def _apply_rope(x, cos, sin):
            x1, x2 = jnp.split(x, 2, axis=-1)
            c = cos[None, :, None, :]
            s = sin[None, :, None, :]
            return jnp.concatenate([x1 * c - x2 * s, x2 * c + x1 * s], axis=-1)
        b, s, d = hidden_states.shape
        residual = hidden_states
        h = _rmsnorm(hidden_states, ln1_w)
        q = (h @ Wq).reshape(b, s, H, HD)
        k = (h @ Wk).reshape(b, s, HKV, HD)
        v = (h @ Wv).reshape(b, s, HKV, HD)
        cos, sin = _rope_cos_sin(s, HD, THETA)
        q = _apply_rope(q, cos, sin)
        k = _apply_rope(k, cos, sin)
        rep = H // HKV
        k = jnp.repeat(k, rep, axis=2)
        v = jnp.repeat(v, rep, axis=2)
        scores = jnp.einsum('bqhd,bkhd->bhqk', q, k) / np.sqrt(HD).astype(np.float32)
        causal = jnp.tril(jnp.ones((s, s), dtype=bool))
        scores = jnp.where(causal[None, None], scores, jnp.finfo(scores.dtype).min)
        attn = jax.nn.softmax(scores, axis=-1)
        ctx = jnp.einsum('bhqk,bkhd->bqhd', attn, v).reshape(b, s, H * HD)
        attn_out = ctx @ Wo
        h = jnp.clip(residual + attn_out, -100.0, 100.0)
        residual = h
        hn = _rmsnorm(h, ln2_w)
        flat = hn.reshape(b * s, d)
        logits = flat @ Wr
        probs = jax.nn.softmax(logits, axis=-1)
        topv, topi = jax.lax.top_k(probs, K)
        topv = topv / jnp.sum(topv, axis=-1, keepdims=True)
        w = jnp.sum(jax.nn.one_hot(topi, E, dtype=flat.dtype) * topv[..., None], axis=1)
        g = jnp.einsum('td,edf->etf', flat, Wg)
        u = jnp.einsum('td,edf->etf', flat, Wu)
        a = jax.nn.silu(g) * u
        o = jnp.einsum('etf,efd->etd', a, Wd)
        moe_out = jnp.einsum('te,etd->td', w, o).reshape(b, s, d)
        out = jnp.clip(residual + moe_out, -100.0, 100.0)
        return out
    x = L0_attn_x
    xn = _layernorm(x, axis=-1)
    x = x + _L0_attn_ref(xn, L0_attn_W_DQ, L0_attn_W_UQ, L0_attn_W_DKV, L0_attn_W_UKV, L0_attn_W_QR, L0_attn_W_KR, L0_attn_W_O, L0_attn_q_norm_w, L0_attn_k_norm_w) + _L0_ffn_ref(xn, L0_ffn_router_weight, L0_ffn_router_bias, L0_ffn_gate_up_proj, L0_ffn_gate_up_proj_bias, L0_ffn_down_proj, L0_ffn_down_proj_bias)
    xn = _layernorm(x, axis=-1)
    x = x + _L1_attn_ref(xn, L1_attn_Wq, L1_attn_Wk, L1_attn_Wv, L1_attn_Wo) + _L1_ffn_ref(xn, L1_ffn_ln1_w, L1_ffn_ln2_w, L1_ffn_Wq, L1_ffn_Wk, L1_ffn_Wv, L1_ffn_Wo, L1_ffn_Wr, L1_ffn_Wg, L1_ffn_Wu, L1_ffn_Wd)
    return x

_drawn_inputs = setup_inputs


def setup_inputs(seed=0):
    import zlib

    import numpy as np

    out = dict(_drawn_inputs(seed))
    spreads = {'L0_attn_q_norm_w': (1.0, 0.6),
     'L0_attn_k_norm_w': (1.0, 0.6),
     'L0_ffn_router_bias': (0.0, 0.1),
     'L0_ffn_gate_up_proj_bias': (0.0, 0.404),
     'L0_ffn_down_proj_bias': (0.0, 0.1)}
    factors = {'L0_attn_W_DQ': 8.0,
     'L0_attn_W_UQ': 8.0,
     'L0_attn_W_DKV': 8.0,
     'L0_attn_W_UKV': 8.0,
     'L0_attn_W_QR': 8.0,
     'L0_attn_W_KR': 8.0,
     'L0_attn_W_O': 8.0,
     'L1_ffn_ln1_w': 8.0,
     'L1_ffn_ln2_w': 8.0,
     'L1_ffn_Wq': 8.0,
     'L1_ffn_Wk': 8.0,
     'L1_ffn_Wv': 8.0,
     'L1_ffn_Wo': 8.0,
     'L1_ffn_Wr': 7.968,
     'L1_ffn_Wg': 6.982,
     'L1_ffn_Wu': 6.92,
     'L1_ffn_Wd': 6.9,
     'L1_attn_Wq': 8.0,
     'L1_attn_Wk': 7.973,
     'L1_attn_Wv': 7.683,
     'L1_attn_Wo': 7.723}
    for name, (base, spread) in spreads.items():
        noise = np.random.default_rng([zlib.crc32(name.encode()), seed]).standard_normal(out[name].shape)
        drawn = base * np.exp(spread * noise) if base else spread * noise
        out[name] = jnp.asarray(drawn.astype(out[name].dtype))
    for name, factor in factors.items():
        out[name] = (out[name] * factor).astype(out[name].dtype)
    return out
```

```python
from contextlib import ExitStack

import numpy as np

import concourse.bass as bass
from concourse import mybir

P = 128
F32 = mybir.dt.float32
F32R = mybir.dt.float32r
BF16 = mybir.dt.bfloat16
I32 = mybir.dt.int32
ALU = mybir.AluOpType
ACT = mybir.ActivationFunctionType
AX = mybir.AxisListType
RMAX = bass.bass_isa.ReduceOp.max

B, T, D = 8, 512, 256
H, HD = 16, 16
HKV = 4
E, F = 8, 512
NT = T // P
DC = D // P
FC = F // P
NP = H // 2
NTOK = B * T
NCH = NTOK // 512
SW = 64
SHIFT = 3 * HD
MASKED = -1.0e30
LN_EPS, QK_EPS, RMS_EPS = 1e-5, 1.1920929e-07, 1e-5
ALPHA, LIMIT = 1.702, 7.0
NEWTON = 21

Q_UNITS = []
K_UNITS = []
for _j in range(2):
    Q_UNITS += [[(_j, 3, 0, 512)], [(_j, 2, 0, 384), (_j, 0, 384, 128)], [(_j, 1, 0, 256)]]
    K_UNITS += [[(_j, 0, 0, 512)], [(_j, 1, 0, 384), (_j, 3, 384, 128)], [(_j, 2, 0, 256)]]
NU = len(Q_UNITS)
PT_AT = {0: 0, 1: 512, 3: 896, 2: 1024}
PT_W = 1280


class Chain:

    def __init__(self, eng, sem):
        self.eng, self.sem, self.n = eng, sem, 0

    def __call__(self, ins):
        self.n += 1
        ins.then_inc(self.sem, 1)
        self.eng.wait_ge(self.sem, self.n)


class Ring:

    def __init__(self, banks):
        self.banks, self.uses, self.at = banks, [], {}

    def add(self, name, engine):
        self.at[name] = len(self.uses)
        self.uses.append(engine)

    def bank(self, name):
        return self.banks[self.at[name] % len(self.banks)]

    def full(self, name):
        return self.at[name] + 1

    def before(self, name):
        n = self.at[name] - len(self.banks)
        if n < 0:
            return None
        return self.uses[n], self.uses[:n + 1].count(self.uses[n])


def bcast(ap, axis, n):
    shape = list(ap.shape)
    shape.insert(axis, n)
    return ap.unsqueeze(axis).broadcast_to(shape)


def program(nc, dram, outs):
    ctx = ExitStack()
    with ctx:
        build(nc, dram, outs, ctx)


def build(nc, dram, outs, ctx):
    def sb(name, shape, dt=F32, stack=ctx):
        if stack is not ctx:
            name = f"{name}_{nc.next_id()}"
        return stack.enter_context(nc.sbuf_tensor(name, shape, dt))

    out = outs["out"]
    x_rows = dram["x"].rearrange("(b t p) d -> b p t d", p=P, t=NT)
    out_rows = out.rearrange("(b t p) d -> b p t d", p=P, t=NT)
    x1_dram = nc.dram_tensor("x1_scratch", [NTOK, D], F32).ap()
    z_dram = nc.dram_tensor("z_scratch", [NTOK, D], F32).ap()
    x1_rows = x1_dram.rearrange("(b t p) d -> b p t d", p=P, t=NT)
    z_rows = z_dram.rearrange("(b t p) d -> b p t d", p=P, t=NT)

    banks = [ctx.enter_context(nc.psum_tensor(f"bank{i}", [P, 512], F32)) for i in range(8)]
    x_banks, gate_bank, up_bank, down_bank = banks[0:2], banks[2], banks[3], banks[4]

    ident = sb("ident", [P, P])
    ident_bf = sb("ident_bf", [P, P], BF16)
    masks_bf = sb("masks_bf", [P, 2, P], BF16)
    halves = sb("halves", [P, 2, 34])
    tie = sb("tie", [P, E, E])
    flag = sb("flag", [P, 8])
    flag_all = sb("flag_all", [P, 8])
    flag_int = sb("flag_int", [P, 1], I32)
    combine = sb("combine", [P, B * NT, E])
    acc = sb("acc", [P, B * NT, D])
    rest_h = sb("rest_h", [P, DC, NTOK], F32R)
    rest_l = sb("rest_l", [P, DC, NTOK], F32R)
    V = sb("V", [P, NT, H, HD + 1])
    xb = sb("xb", [P, NT, D])
    xT = sb("xT", [P, DC, T])
    qkr = sb("qkr", [P, NT, 3, D])
    small = sb("small", [P, 64])
    rt = sb("rt", [P, 8, NT * E])

    def sem_maker():
        made = []

        def new(name):
            s = nc.alloc_semaphore(f"{name}_{nc.next_id()}")
            made.append(s)
            return s

        def done():
            nc.clear_and_free_semaphores(made)
            nc.all_engine_barrier()
        return new, done

    def setup():
        new, done = sem_maker()
        with ExitStack() as st:
            masks = sb("masks", [P, 2, P], F32, st)
            loaded, cast, filled = new("loaded"), new("cast"), new("filled")
            with nc.Block() as block:
                @block.sync
                def _(sp):
                    sp.dma_start(ident[:, :], dram["c_ident"]).then_inc(loaded, 16)
                    sp.dma_start(masks[:, :, :], dram["c_masks"]).then_inc(loaded, 16)
                    sp.dma_start(halves[:, :, :], dram["c_halves"]).then_inc(loaded, 16)
                    sp.dma_start(tie[:, :, :], dram["c_tie"]).then_inc(loaded, 16)
                    for b in range(B):
                        sp.dma_start(acc[:, NT * b:NT * (b + 1), :], x_rows[b]).then_inc(loaded, 16)
                    sp.wait_ge(loaded, 16 * (4 + B))

                @block.vector
                def _(dve):
                    dve.memset(V[:, :, :, HD:HD + 1], 1.0).then_inc(filled, 1)
                    dve.memset(flag[:, :], 0.0).then_inc(filled, 1)
                    dve.wait_ge(loaded, 16 * (4 + B))
                    dve.tensor_copy(ident_bf[:, :], ident[:, :]).then_inc(cast, 1)
                    dve.tensor_copy(masks_bf[:, :, :], masks[:, :, :]).then_inc(cast, 1)
                    dve.wait_ge(cast, 2)
                    dve.wait_ge(filled, 2)
            done()

    def fold(weights):
        new, done = sem_maker()
        with ExitStack() as st:
            dq = sb("f_dq", [P, P], F32, st)
            uq = sb("f_uq", [P, HD], F32, st)
            dkv = sb("f_dkv", [P, 2, P], F32, st)
            ukv = sb("f_ukv", [P, 2, 2 * HD], F32, st)
            kr = sb("f_kr", [64, P], F32, st)
            qr = sb("f_qr", [64, HD], F32, st)
            wo = sb("f_wo", [HD, HD], F32, st)
            av = sb("f_av", [HD, P], F32, st)
            four = sb("f_four", [P, 4, HD], F32, st)
            bm = sb("f_bm", [P, 8], F32, st)
            loaded, products, copied, value = new("loaded"), new("products"), new("copied"), new("value")
            ps, pv = banks[0], banks[1]
            with nc.Block() as block:
                @block.sync
                def _(sp):
                    for to, name in ((dq, "dq"), (uq, "uq"), (dkv, "dkv"), (ukv, "ukv"), (kr, "kr"),
                                     (qr, "qr"), (wo, "wo"), (bm, "c_block")):
                        sp.dma_start(to[tuple(slice(None) for _ in to.shape)], dram[name]).then_inc(loaded, 16)

                @block.tensor
                def _(pe):
                    pe.wait_ge(loaded, 16 * 8)
                    pe.matmul(ps[:, 0:16], dq[:, :], uq[:, :], start=True, stop=True)
                    for c in range(2):
                        pe.matmul(ps[:, 16:32], dkv[:, c, :], ukv[:, c, 0:HD], start=(c == 0), stop=(c == 1))
                    pe.matmul(ps[:, 32:48], kr[:, :], qr[:, :], start=True, stop=True)
                    for c in range(2):
                        mm = pe.matmul(pv[0:HD, 0:P], ukv[:, c, HD:2 * HD], dkv[:, c, :],
                                       start=(c == 0), stop=(c == 1))
                    mm.then_inc(products, 1)
                    pe.wait_ge(value, 1)
                    pe.matmul(ps[:, 48:64], av[:, :], wo[:, :], start=True, stop=True).then_inc(products, 1)

                @block.vector
                def _(dve):
                    dve.wait_ge(products, 1)
                    dve.tensor_copy(av[:, :], pv[0:HD, 0:P]).then_inc(value, 1)
                    dve.wait_ge(products, 2)
                    dve.tensor_copy(four[:, :, :], ps[:, 0:64].rearrange("p (m o) -> p m o", m=4)).then_inc(copied, 1)
                    dve.wait_ge(copied, 1)
                    for m in range(4):
                        dve.tensor_tensor(weights[:, m, :].rearrange("p (h o) -> p h o", o=HD),
                                          bcast(four[:, m, :], 1, 8), bcast(bm[:, :], 2, HD),
                                          ALU.mult).then_inc(copied, 1)
                    dve.wait_ge(copied, 5)
            done()

    def rms_rows(dve, act, chain, sem_in, sem_out):
        pass

    def router(dve, chain, logits, k, exp_ready, exp_done):
        lg = rt[:, 0, :].rearrange("p (t e) -> p t e", e=E)
        return lg

    def iteration(it, kind, moe, mem, general=False):
        new, done = sem_maker()
        attn = kind in ("mla", "gqa", "spm")
        routed = {"none": 4, "gqa": 2}.get(kind, 0)
        s_banks = banks[5:8] if moe else banks[2:8]
        rows = slice(None)
        at = bass.ds(it * NT, NT)
        at_tok = bass.ds(it * T, T)

        X = Ring(x_banks)
        X.add("Tx0", "act")
        X.add("Tx1", "act")
        if attn:
            for t in range(NT):
                X.add(f"proj{t}a", "act")
                if kind != "gqa":
                    X.add(f"proj{t}b", "act")
            X.add("Tq0", "act")
            X.add("Tk0", "dve")
            for p in range(NP):
                X.add(f"Ta{p}", "act")
                if p + 1 < NP:
                    X.add(f"Tq{p + 1}", "act")
                    X.add(f"Tk{p + 1}", "dve")
                X.add(f"O{p}", "act")
                X.add(f"N{p}", "dve")
            if kind != "mla":
                for n, who in (("Tc0", "act"), ("Tc1", "act"), ("Y0", "dve"), ("Y1", "dve")):
                    X.add(n, who)
        if kind == "gqa":
            X.add("Th0", "dve")
            X.add("Th1", "dve")
        if kind == "none":
            X.uses[0] = X.uses[1] = "dve"
        if routed:
            X.add("R", "dve")
        if kind == "none":
            for n, who in (("Cc", "act"), ("B0", "dve"), ("B1", "dve")):
                X.add(n, who)
        S = Ring(s_banks)
        if attn:
            for u in range(NU):
                S.add(("q", 0, u), "dve")
            for p in range(NP):
                for u in range(NU):
                    S.add(("k", p, u), "act")
                if p + 1 < NP:
                    for u in range(NU):
                        S.add(("q", p + 1, u), "dve")

        x_full, x_act, x_dve = new("x_full"), new("x_act"), new("x_dve")
        s_full, s_act, s_dve = new("s_full"), new("s_act"), new("s_dve")
        x_rel = {"act": x_act, "dve": x_dve}
        s_rel = {"act": s_act, "dve": s_dve}
        dve_step, act_step, pool_step = new("dve_step"), new("act_step"), new("pool_step")
        loaded, stored, x1_saved = new("loaded"), new("stored"), new("x1_saved")
        var_ready, std_ready, xn_ready = new("var_ready"), new("std_ready"), new("xn_ready")
        ms_ready, rms_ready = new("ms_ready"), new("rms_ready")
        sq_ready, xT_ready = new("sq_ready"), new("xT_ready")
        proj_ready, qk_ready = new("proj_ready"), new("qk_ready")
        qk_ms, qk_std = new("qk_ms"), new("qk_std")
        stack_ready, qsT_ready, ksT_ready = new("stack_ready"), new("qsT_ready"), new("ksT_ready")
        shift_ready, qaT_ready = new("shift_ready"), new("qaT_ready")
        o_ready, ctx_ready = new("o_ready"), new("ctx_ready")
        cT_ready, h_ready, hms_ready, hstd_ready, hn_ready = (
            new("cT_ready"), new("h_ready"), new("hms_ready"), new("hstd_ready"), new("hn_ready"))
        rest_hi, lg_ready, exp_ready, comb_ready, cc_ready = (
            new("rest_hi"), new("lg_ready"), new("exp_ready"), new("comb_ready"), new("cc_ready"))
        if moe:
            gu_high, gu_split, dn_loaded, dn_high, dn_split, gu_next = (
                new("gu_high"), new("gu_split"), new("dn_loaded"), new("dn_high"), new("dn_split"), new("gu_next"))
            g_full, g_used, u_full, u_used = new("g_full"), new("g_used"), new("u_full"), new("u_used")
            th_ready, a_ready, ah_ready, al_ready = new("th_ready"), new("a_ready"), new("ah_ready"), new("al_ready")
            y_full, y_used, picked = new("y_full"), new("y_used"), new("picked")

        ctxt = qkr[:, :, 2, :]
        norm_in = xb

        block = nc.Block()
        with block as block:
            @block.sync
            def _(sp):
                if kind in ("mla", "spm"):
                    src = x_rows if kind == "mla" else x1_rows
                    sp.dma_start(xb[:, :, :], src[it]).then_inc(loaded, 16)
                if kind == "gqa":
                    sp.dma_start(x1_rows[it], acc[:, at, :]).then_inc(x1_saved, 16)
                if moe:
                    sp.wait_ge(gu_split, 4)
                    sp.dma_start(mem["raw"][:, 0:FC * D], mem["dn_dram"][it]).then_inc(dn_loaded, 16)
                    sp.wait_ge(dn_split, 2)
                    sp.dma_start(mem["raw"][:, :], mem["gu_dram"][it]).then_inc(gu_next, 16)
                if kind == "spm":
                    sp.wait_ge(x_full, X.full("Tx1"))
                    sp.dma_start(xb[:, :, :], x1_rows[it]).then_inc(loaded, 16)
                    sp.wait_ge(h_ready, 2)
                    sp.dma_start(z_rows[it], qkr[:, :, 0, :]).then_inc(stored, 16)
                    sp.wait_ge(stored, 16)
                if kind == "gqa":
                    sp.wait_ge(x1_saved, 16)
                if moe:
                    sp.wait_ge(gu_next, 16)

            @block.gpsimd
            def _(pool):
                chain = Chain(pool, pool_step)

                def low(m):
                    j = m % FC
                    pool.wait_ge(ah_ready, m + 1)
                    pool.tensor_tensor(mem["al"][:, j, :], mem["t"][m % 2][:, :], mem["ah"][:, j, :].bitcast(F32),
                                       ALU.subtract).then_inc(al_ready, 1)

                def stack(p):
                    if p == 0:
                        pool.wait_ge(qk_ready, 1)
                    if p >= 1:
                        pool.wait_ge(x_full, X.full(f"Tk{p - 1}"))
                    if p >= 2:
                        pool.wait_ge(x_full, X.full(f"Ta{p - 2}"))
                    qs, ks = mem["qst"][p % 2], mem["kst"]
                    q = qkr[:, :, 0, 2 * HD * p:2 * HD * (p + 1)].rearrange("p t (j d) -> p t j d", j=2)
                    if kind == "gqa":
                        g = p // (NP // HKV)
                        k = bcast(qkr[:, :, 1, HD * g:HD * (g + 1)], 2, 2)
                    else:
                        k = qkr[:, :, 1, 2 * HD * p:2 * HD * (p + 1)].rearrange("p t (j d) -> p t j d", j=2)
                    pool.tensor_copy(qs[:, :, :, 0:HD].bitcast(F32R), q).then_inc(pool_step, 1)
                    pool.tensor_copy(ks[:, :, :, 0:HD].bitcast(F32R), k).then_inc(pool_step, 1)
                    chain.n += 2
                    pool.wait_ge(pool_step, chain.n)
                    pool.tensor_tensor(qs[:, :, :, HD:2 * HD], q, qs[:, :, :, 0:HD], ALU.subtract).then_inc(pool_step, 1)
                    pool.tensor_tensor(ks[:, :, :, 2 * HD:3 * HD], k, ks[:, :, :, 0:HD], ALU.subtract).then_inc(pool_step, 1)
                    pool.tensor_copy(qs[:, :, :, 2 * HD:3 * HD], qs[:, :, :, 0:HD]).then_inc(pool_step, 1)
                    chain.n += 3
                    pool.wait_ge(pool_step, chain.n)
                    pool.tensor_copy(ks[:, :, :, HD:2 * HD], ks[:, :, :, 0:HD]).then_inc(stack_ready, 1)

                if attn:
                    if moe:
                        low(0)
                    stack(0)
                    if moe:
                        low(1)
                        low(2)
                    stack(1)
                    for p in range(NP):
                        c = p + 1
                        if moe:
                            low(FC * c - 1)
                        if p + 2 < NP:
                            stack(p + 2)
                        if moe and c < NCH:
                            for j in range(FC - 1):
                                low(FC * c + j)

            @block.scalar
            def _(act):
                if moe:
                    for q in range(4):
                        act.activation(mem["guh"][:, 512 * q:512 * (q + 1)], mem["raw"][:, 512 * q:512 * (q + 1)],
                                       ACT.Copy).then_inc(gu_high, 1)
                act.wait_ge(var_ready, 1)
                act.activation(small[:, 4:8], small[:, 0:4], ACT.Sqrt).then_inc(std_ready, 1)
                if kind == "gqa":
                    act.wait_ge(xn_ready, 4)
                    for t in range(NT):
                        act.activation(ctxt[:, t, :], xb[:, t, :], ACT.Square,
                                       accum_out=small[:, 16 + t:17 + t]).then_inc(sq_ready, 1)
                    act.wait_ge(ms_ready, 1)
                    act.activation(small[:, 20:24], small[:, 16:20], ACT.Sqrt).then_inc(rms_ready, 1)

                def gate(m):
                    if mem["layer"] == 0:
                        act.wait_ge(g_used, m + 1)
                        if m >= 1:
                            act.wait_ge(a_ready, m)
                        act.activation(mem["th"][:, :], mem["gc"][:, :], ACT.Tanh,
                                       scale=ALPHA / 2).then_inc(th_ready, 1)
                    else:
                        act.wait_ge(g_full, m + 1)
                        if m >= 2:
                            act.wait_ge(a_ready, m - 1)
                        act.activation((mem["gc"], mem["th"])[m % 2][:, :], gate_bank[:, :],
                                       ACT.Silu).then_inc(g_used, 1)

                def high(m):
                    act.wait_ge(a_ready, m + 1)
                    if m >= FC:
                        act.wait_ge(y_full, 2 * (m // FC))
                    act.activation(mem["ah"][:, m % FC, :], mem["t"][m % 2][:, :], ACT.Copy).then_inc(ah_ready, 1)

                def down_high():
                    act.wait_ge(dn_loaded, 16)
                    for q in range(2):
                        act.activation(mem["dnh"][:, 512 * q:512 * (q + 1)], mem["raw"][:, 512 * q:512 * (q + 1)],
                                       ACT.Copy).then_inc(dn_high, 1)

                def take(name, to, frm, scale=1.0, sem=None, release=True):
                    act.wait_ge(x_full, X.full(name))
                    return act.activation(to, frm, ACT.Copy, scale=scale)

                if moe:
                    gate(0)
                for c in range(DC):
                    act.wait_ge(x_full, X.full(f"Tx{c}"))
                    if kind == "gqa":
                        act.activation(xT[:, c, :], X.bank(f"Tx{c}")[:, :], ACT.Copy,
                                       scale=mem["ln"][:, c:c + 1]).then_inc(x_act, 1)
                    elif kind == "none":
                        act.activation(xT[:, c, :], X.bank(f"Tx{c}")[:, :], ACT.Copy).then_inc(xT_ready, 1)
                        act.activation(rest_h[:, c, at_tok], X.bank(f"Tx{c}")[:, :], ACT.Copy).then_inc(rest_hi, 1)
                    else:
                        act.activation(xT[:, c, :], X.bank(f"Tx{c}")[:, :], ACT.Copy).then_inc(x_act, 1)
                if moe:
                    down_high()
                    high(0)
                    gate(1)
                if attn:
                    scale = 1.0 / 4.0
                    for t in range(NT):
                        act.wait_ge(x_full, X.full(f"proj{t}a"))
                        a = X.bank(f"proj{t}a")
                        if kind == "mla":
                            for c, n in enumerate("ab"):
                                a = X.bank(f"proj{t}{n}")
                                act.wait_ge(x_full, X.full(f"proj{t}{n}"))
                                act.activation(qkr[:, t, :, P * c:P * (c + 1)],
                                               a[:, 0:3 * P].rearrange("p (m o) -> p m o", m=3), ACT.Copy).then_inc(proj_ready, 1)
                                act.activation(V[:, t, 8 * c:8 * (c + 1), 0:HD],
                                               a[:, 3 * P:4 * P].rearrange("p (h o) -> p h o", o=HD), ACT.Copy).then_inc(x_act, 1)
                        elif kind == "spm":
                            act.activation(qkr[:, t, 0, :], a[:, 0:D], ACT.Copy, scale=scale).then_inc(proj_ready, 1)
                            act.activation(qkr[:, t, 1, :], a[:, D:2 * D], ACT.Copy).then_inc(x_act, 1)
                            v = X.bank(f"proj{t}b")
                            act.wait_ge(x_full, X.full(f"proj{t}b"))
                            act.activation(V[:, t, :, 0:HD], v[:, 0:D].rearrange("p (h o) -> p h o", o=HD),
                                           ACT.Copy).then_inc(x_act, 1)
                        else:
                            act.activation(qkr[:, t, 0, :], a[:, 0:D], ACT.Copy, scale=scale).then_inc(proj_ready, 1)
                            act.activation(qkr[:, t, 1, 0:64], a[:, D:D + 64], ACT.Copy).then_inc(proj_ready, 1)
                            act.activation(V[:, t, 0:HKV, 0:HD],
                                           a[:, D + 64:D + 128].rearrange("p (h o) -> p h o", o=HD),
                                           ACT.Copy).then_inc(x_act, 1)
                    if kind == "mla":
                        act.wait_ge(qk_ms, 1)
                        act.activation(mem["qkn"][:, :], mem["qkn"][:, :], ACT.Sqrt).then_inc(qk_std, 1)
                    if moe:
                        high(1)
                        gate(2)
                        high(2)
                        gate(3)

                    def take_q(p):
                        act.wait_ge(x_full, X.full(f"Tq{p}"))
                        act.activation(mem["qsT"][:, :], X.bank(f"Tq{p}")[:, :], ACT.Copy).then_inc(x_act, 1)

                    def probabilities(p):
                        if p >= 1:
                            act.wait_ge(x_full, X.full(f"O{p - 1}"))
                        for u in range(NU):
                            unit, bank = K_UNITS[u], S.bank(("k", p, u))
                            act.wait_ge(s_full, S.full(("k", p, u)))
                            j, first = unit[0][0], PT_AT[unit[0][1]]
                            width = sum(w for _, _, _, w in unit)
                            to, frm = mem["pt"][:, j, first:first + width], bank[:, 0:width]
                            act.activation(to, frm, ACT.Relu if kind == "spm" else ACT.Exp).then_inc(s_act, 1)

                    take_q(0)
                    for p in range(NP):
                        c = p + 1
                        act.wait_ge(x_full, X.full(f"Ta{p}"))
                        act.activation(mem["qaT"][:, :], X.bank(f"Ta{p}")[:, :], ACT.Copy).then_inc(x_act, 1)
                        if p + 1 < NP:
                            take_q(p + 1)
                        if moe:
                            high(FC * c - 1)
                        if moe and c < NCH:
                            gate(FC * c)
                        probabilities(p)
                        if moe and c < NCH:
                            gate(FC * c + 1)
                            high(FC * c)
                            high(FC * c + 1)
                        act.wait_ge(x_full, X.full(f"O{p}"))
                        act.activation(mem["oT"][:, :], X.bank(f"O{p}")[:, :], ACT.Copy).then_inc(x_act, 1)
                        if moe and c < NCH:
                            gate(FC * c + 2)
                            high(FC * c + 2)
                            gate(FC * c + 3)
                    if kind != "mla":
                        for c in range(DC):
                            act.wait_ge(x_full, X.full(f"Tc{c}"))
                            act.activation(xT[:, c, :], X.bank(f"Tc{c}")[:, :], ACT.Copy).then_inc(x_act, 1)
                if kind == "gqa":
                    act.wait_ge(h_ready, 4)
                    for t in range(NT):
                        act.activation(qkr[:, t, 0, :], ctxt[:, t, :], ACT.Square,
                                       accum_out=small[:, 32 + t:33 + t]).then_inc(sq_ready, 1)
                    act.wait_ge(hms_ready, 1)
                    act.activation(small[:, 36:40], small[:, 32:36], ACT.Sqrt).then_inc(hstd_ready, 1)
                    for c in range(DC):
                        act.wait_ge(x_full, X.full(f"Th{c}"))
                        act.activation(xT[:, c, :], X.bank(f"Th{c}")[:, :], ACT.Copy,
                                       scale=mem["ln"][:, 2 + c:3 + c]).then_inc(xT_ready, 1)
                        act.wait_ge(xT_ready, c + 1)
                        act.activation(rest_h[:, c, at_tok], xT[:, c, :], ACT.Copy).then_inc(rest_hi, 1)
                if routed:
                    act.wait_ge(lg_ready, 1)
                    act.activation(rt[:, 5, :], rt[:, 4, :], ACT.Exp).then_inc(exp_ready, 1)
                if kind == "none":
                    act.wait_ge(x_full, X.full("Cc"))
                    act.activation(mem["cT"][:, :], X.bank("Cc")[0:E, :], ACT.Copy).then_inc(x_act, 1)

            @block.vector
            def _(dve):
                chain = Chain(dve, dve_step)
                if moe:
                    for q in range(4):
                        dve.wait_ge(gu_high, q + 1)
                        sl = slice(512 * q, 512 * (q + 1))
                        dve.tensor_tensor(mem["gul"][:, sl], mem["raw"][:, sl], mem["guh"][:, sl].bitcast(F32),
                                          ALU.subtract).then_inc(gu_split, 1)
                    dve.tensor_copy(mem["ce"][:, :], combine[:, :, bass.ds(it, 1)]).then_inc(picked, 1)
                    if mem["layer"] == 0:
                        dve.tensor_copy(mem["be"][:, :], mem["biases"][:, bass.ds(it, 1), :]).then_inc(picked, 1)
                if kind in ("mla", "spm"):
                    dve.wait_ge(loaded, 16)
                    src = [xb[:, t, :] for t in range(NT)]
                else:
                    src = [acc[:, bass.ds(it * NT + t, 1), :] for t in range(NT)]
                for t in range(NT):
                    dve.bn_stats(small[:, 40 + 6 * t:46 + 6 * t] if t < 4 else None, src[t]).then_inc(dve_step, 1)
                chain.n += NT
                dve.wait_ge(dve_step, chain.n)
                for t in range(NT):
                    dve.bn_aggr(small[:, 8 + 2 * t:10 + 2 * t], small[:, 40 + 6 * t:46 + 6 * t]).then_inc(dve_step, 1)
                chain.n += NT
                dve.wait_ge(dve_step, chain.n)
                mean_var = small[:, 8:16].rearrange("p (t two) -> p t two", two=2)
                dve.tensor_scalar(small[:, 0:4], mean_var[:, :, 1], LN_EPS, None, ALU.add).then_inc(var_ready, 1)
                dve.wait_ge(std_ready, 1)
                chain(dve.reciprocal(small[:, 4:8], small[:, 4:8]))
                for t in range(NT):
                    dve.tensor_scalar(xb[:, t, :], src[t], small[:, 8 + 2 * t:9 + 2 * t], small[:, 4 + t:5 + t],
                                      ALU.subtract, ALU.mult).then_inc(xn_ready, 1)
                if kind == "gqa":
                    dve.wait_ge(sq_ready, NT)
                    dve.tensor_scalar(small[:, 16:20], small[:, 16:20], 1.0 / D, RMS_EPS, ALU.mult,
                                      ALU.add).then_inc(ms_ready, 1)
                    dve.wait_ge(rms_ready, 1)
                    dve.wait_ge(xn_ready, NT)
                    chain(dve.reciprocal(small[:, 24:28], small[:, 20:24]))
                    for t in range(NT):
                        dve.tensor_scalar(ctxt[:, t, :], xb[:, t, :], small[:, 24 + t:25 + t], None,
                                          ALU.mult).then_inc(xn_ready, 1)

                def hidden(m):
                    j = m % FC
                    t = mem["t"][m % 2]
                    if m == 0 and mem["layer"] == 0:
                        dve.wait_ge(picked, 2)
                    if mem["layer"] == 0:
                        dve.wait_ge(g_full, m + 1)
                        if m >= 1:
                            dve.wait_ge(a_ready, m)
                        dve.tensor_scalar(mem["gc"][:, :], gate_bank[:, :], mem["be"][:, j:j + 1], LIMIT,
                                          ALU.add, ALU.min).then_inc(g_used, 1)
                    dve.wait_ge(u_full, m + 1)
                    if m >= 2:
                        dve.wait_ge(al_ready, m - 1)
                    if mem["layer"] == 0:
                        dve.tensor_scalar(t[:, :], up_bank[:, :], mem["be"][:, FC + j:FC + j + 1], LIMIT + 1.0,
                                          ALU.add, ALU.min).then_inc(u_used, 1)
                        dve.wait_ge(th_ready, m + 1)
                        chain(dve.scalar_tensor_tensor(mem["gc"][:, :], mem["th"][:, :], 1.0, mem["gc"][:, :],
                                                       ALU.add, ALU.mult))
                        dve.wait_ge(u_used, m + 1)
                        dve.scalar_tensor_tensor(t[:, :], t[:, :], 1.0 - LIMIT, mem["gc"][:, :],
                                                 ALU.max, ALU.mult).then_inc(a_ready, 1)
                    else:
                        dve.wait_ge(g_used, m + 1)
                        dve.tensor_tensor(t[:, :], (mem["gc"], mem["th"])[m % 2][:, :], up_bank[:, :],
                                          ALU.mult).then_inc(a_ready, 1)

                def down_low():
                    for q in range(2):
                        dve.wait_ge(dn_high, q + 1)
                        sl = slice(512 * q, 512 * (q + 1))
                        dve.tensor_tensor(mem["dnl"][:, sl], mem["raw"][:, sl], mem["dnh"][:, sl].bitcast(F32),
                                          ALU.subtract).then_inc(dn_split, 1)

                def add_down(c, half):
                    if c == 0 and half == 0:
                        dve.wait_ge(picked, 1)
                    dve.wait_ge(y_full, 2 * c + half + 1)
                    for i in range(2):
                        n = NT * c + 2 * half + i
                        ins = dve.scalar_tensor_tensor(acc[:, n, :], down_bank[:, D * i:D * (i + 1)],
                                                       mem["ce"][:, n:n + 1], acc[:, n, :], ALU.mult, ALU.add)
                    ins.then_inc(y_used, 1)

                if moe:
                    hidden(0)
                    down_low()
                    hidden(1)

                if kind == "mla":
                    dve.wait_ge(proj_ready, 2 * NT)
                    both = qkr[:, :, 0:2, :]
                    flat = mem["sq"][:, :]
                    for t in range(NT):
                        dve.tensor_tensor(flat[:, 0:2 * D].rearrange("p (m o) -> p m o", m=2), qkr[:, t, 0:2, :],
                                          qkr[:, t, 0:2, :], ALU.mult).then_inc(dve_step, 1)
                        chain.n += 1
                        dve.wait_ge(dve_step, chain.n)
                        chain(dve.tensor_reduce(mem["qkn"][:, 2 * H * t:2 * H * (t + 1)],
                                                flat[:, 0:2 * D].rearrange("p (h o) -> p h o", o=HD), AX.X, ALU.add))
                    dve.tensor_scalar(mem["qkn"][:, :], mem["qkn"][:, :], 1.0 / HD, QK_EPS, ALU.mult,
                                      ALU.add).then_inc(qk_ms, 1)
                    dve.wait_ge(qk_std, 1)
                    chain(dve.reciprocal(mem["qkn"][:, :], mem["qkn"][:, :]))
                    r = mem["qkn"][:, :].rearrange("p (t m h) -> p t m h", t=NT, m=2)
                    chain(dve.tensor_scalar(r[:, :, 0, :], r[:, :, 0, :], 0.25, None, ALU.mult))
                    for t in range(NT):
                        v = qkr[:, t, 0:2, :].rearrange("p m (h o) -> p (m h) o", o=HD)
                        dve.tensor_tensor(v, v, bcast(mem["qkn"][:, 2 * H * t:2 * H * (t + 1)], 2, HD),
                                          ALU.mult).then_inc(dve_step, 1)
                    chain.n += NT
                    dve.wait_ge(dve_step, chain.n)
                    for t in range(NT):
                        v = qkr[:, t, 0:2, :].rearrange("p m (h o) -> p m h o", o=HD)
                        w = bcast(mem["qkw"][:, :, :], 2, H)
                        dve.tensor_tensor(v, v, w, ALU.mult).then_inc(dve_step, 1)
                    chain.n += NT
                    dve.wait_ge(dve_step, chain.n)
                    dve.tensor_tensor(qkr[:, :, 1, :], qkr[:, :, 1, :], qkr[:, :, 2, :], ALU.add).then_inc(qk_ready, 1)
                if kind == "gqa":
                    dve.wait_ge(proj_ready, 2 * NT)
                    dve.wait_ge(x_act, X.before("Ta0")[1] - 1 if False else 2 + NT)
                    for part, heads in ((0, H), (1, HKV)):
                        for t in range(NT):
                            v = qkr[:, t, part, 0:HD * heads].rearrange("p (h s o) -> p h s o", s=2, o=HD // 2)
                            cs = mem["cs"][:, t, 0, :]
                            sn = mem["cs"][:, t, 1, :]
                            tmp = mem["sq"][:, 0:HD * heads].rearrange("p (h s o) -> p h s o", s=2, o=HD // 2)
                            dve.tensor_tensor(tmp[:, :, 0, :], v[:, :, 1, :], bcast(sn, 1, heads),
                                              ALU.mult).then_inc(dve_step, 1)
                            dve.tensor_tensor(tmp[:, :, 1, :], v[:, :, 0, :], bcast(sn, 1, heads),
                                              ALU.mult).then_inc(dve_step, 1)
                            chain.n += 2
                            dve.wait_ge(dve_step, chain.n)
                            flat_v = qkr[:, t, part, 0:HD * heads].rearrange("p (h o) -> p h o", o=HD // 2)
                            chain(dve.tensor_tensor(flat_v, flat_v, bcast(cs, 1, 2 * heads), ALU.mult))
                            dve.tensor_tensor(v[:, :, 0, :], v[:, :, 0, :], tmp[:, :, 0, :],
                                              ALU.subtract).then_inc(dve_step, 1)
                            chain(dve.tensor_tensor(v[:, :, 1, :], v[:, :, 1, :], tmp[:, :, 1, :], ALU.add))
                            chain.n += 1
                            dve.wait_ge(dve_step, chain.n)
                    dve.tensor_scalar(small[:, 0:1], small[:, 0:1], 1.0, None, ALU.mult).then_inc(qk_ready, 1)
                if kind == "spm":
                    dve.wait_ge(x_act, X.before("Ta0")[1] if False else 2 + 2 * NT)
                    dve.wait_ge(proj_ready, NT)
                    dve.tensor_scalar(small[:, 0:1], small[:, 0:1], 1.0, None, ALU.mult).then_inc(qk_ready, 1)
                if moe:
                    hidden(2)
                    hidden(3)

                def take_k(p):
                    dve.wait_ge(x_full, X.full(f"Tk{p}"))
                    dve.tensor_copy(mem["ksT"][p % 2][:, :], X.bank(f"Tk{p}")[:, :]).then_inc(x_dve, 1)

                def shift(p, between=None):
                    st, qs = mem["st"], mem["qst"][p % 2]
                    top = mem.get("top")
                    held = []
                    for u in range(NU):
                        if u == NU // 2 and between:
                            between()
                        bank = S.bank(("q", p, u))
                        dve.wait_ge(s_full, S.full(("q", p, u)))
                        for n, (j, t, first, width) in enumerate(Q_UNITS[u]):
                            last = n == len(Q_UNITS[u]) - 1
                            r = 2 * t + j
                            if kind == "spm":
                                ins = dve.max(top[:, 0, r, :], bank[:, first:first + width])
                            else:
                                ins = dve.reduce_max(st[:, 0, r:r + 1], bank[:, first:first + width], AX.X)
                            if last and not general:
                                ins.then_inc(s_dve, 1)
                            else:
                                ins.then_inc(dve_step, 1)
                                chain.n += 1
                            held.append((r, bank, first, width))
                    dve.wait_ge(dve_step, chain.n)
                    if not general:
                        dve.wait_ge(s_dve, S.uses[:S.full(("q", p, NU - 1))].count("dve"))
                    if kind != "spm":
                        chain(dve.tensor_scalar(st[:, 1, :], st[:, 0, :], -1.0, None, ALU.mult))
                    else:
                        z = top[:, 0, :, :]
                        dve.tensor_tensor(top[:, 1, :, :], z, z[:, :, 0:1].broadcast_to([P, 8, 8]), ALU.subtract).then_inc(dve_step, 1)
                        chain.n += 1
                        dve.wait_ge(dve_step, chain.n)
                        rel = top[:, 1, :, :].rearrange("p r k -> p (r k)")
                        chain(dve.tensor_tensor_scan(top[:, 2, :, :].rearrange("p r k -> p (r k)"),
                                                     mem["keep"][:, 0, :], rel, 0.0, ALU.mult, ALU.add))
                        chain(dve.tensor_tensor(top[:, 3, :, :].rearrange("p r k -> p (r k)"), rel,
                                                mem["keep"][:, 1, :], ALU.mult))
                        chain(dve.scalar_tensor_tensor(top[:, 4, :, :].rearrange("p r k -> p (r k)"),
                                                       top[:, 3, :, :].rearrange("p r k -> p (r k)"), 1.0,
                                                       top[:, 2, :, :].rearrange("p r k -> p (r k)"), ALU.add, ALU.is_gt))
                        chain(dve.tensor_reduce(st[:, 2, :], top[:, 4, :, :], AX.X, ALU.add))
                        chain(dve.tensor_tensor(top[:, 3, :, :], top[:, 1, :, :], top[:, 4, :, :], ALU.mult))
                        chain(dve.tensor_reduce(st[:, 3, :], top[:, 3, :, :], AX.X, ALU.add))
                        chain(dve.reciprocal(st[:, 4, :], st[:, 2, :]))
                        chain(dve.scalar_tensor_tensor(st[:, 5, :], st[:, 3, :], -1.0, st[:, 4, :], ALU.add, ALU.mult))
                        chain(dve.scalar_tensor_tensor(st[:, 1, :], st[:, 5, :], -1.0, z[:, :, 0], ALU.mult, ALU.subtract))
                        if not general:
                            chain(dve.tensor_tensor(flag[:, :], flag[:, :], top[:, 4, :, 7], ALU.max))
                        else:
                            newton(p, held, st)
                    rv = st[:, 1, :].rearrange("p (t j) -> p t j", j=2)
                    chain(dve.tensor_copy(qs[:, :, :, SHIFT].bitcast(F32R), rv))
                    dve.tensor_tensor(qs[:, :, :, SHIFT + 1], rv, qs[:, :, :, SHIFT], ALU.subtract).then_inc(shift_ready, 1)

                def newton(p, held, st):
                    with dve.Fori(0, NEWTON):
                        for r, bank, first, width in held:
                            region = bank[:, first:first + width]
                            junk = mem["junk"][:, 0:width]
                            dve.scalar_tensor_tensor(junk, region, st[:, 1, r:r + 1], mem["zero"][:, 0:width],
                                                     ALU.add, ALU.max, accum_out=st[:, 2, r:r + 1])
                            dve.drain()
                            dve.scalar_tensor_tensor(junk, region, st[:, 1, r:r + 1], mem["zero"][:, 0:width],
                                                     ALU.add, ALU.is_gt, accum_out=st[:, 3, r:r + 1])
                            dve.drain()
                        dve.reciprocal(st[:, 4, :], st[:, 3, :])
                        dve.drain()
                        dve.scalar_tensor_tensor(st[:, 5, :], st[:, 2, :], -1.0, st[:, 4, :], ALU.add, ALU.mult)
                        dve.drain()
                        dve.tensor_tensor(st[:, 1, :], st[:, 1, :], st[:, 5, :], ALU.subtract)
                        dve.drain()
                    for u in range(NU):
                        dve.tensor_copy(st[:, 6, u:u + 1], st[:, 1, u:u + 1]).then_inc(s_dve, 1)

                def heads_out(p):
                    dve.wait_ge(x_full, X.full(f"N{p}"))
                    o = X.bank(f"N{p}")[:, 0:4 * 64].rearrange("p (t n) -> p t n", t=NT)[:, :, 0:34] \
                        .rearrange("p t (j d) -> p t j d", j=2)
                    to = ctxt[:, :, 2 * HD * p:2 * HD * (p + 1)].rearrange("p t (j d) -> p t j d", j=2)
                    if kind == "spm":
                        dve.tensor_copy(to, o[:, :, :, 0:HD]).then_inc(x_dve, 1)
                    else:
                        rec = mem["rec"][:, :].rearrange("p (t j) -> p t j", j=2)
                        chain(dve.reciprocal(rec, o[:, :, :, HD]))
                        dve.tensor_tensor(to, o[:, :, :, 0:HD], bcast(rec, 3, HD), ALU.mult).then_inc(x_dve, 1)

                if attn:
                    take_k(0)
                    shift(0)
                    for p in range(NP):
                        c = p + 1
                        if p + 1 < NP:
                            take_k(p + 1)
                        if moe and c < NCH:
                            hidden(FC * c)
                        if moe:
                            add_down(c - 1, 0)
                        if moe and c < NCH:
                            hidden(FC * c + 1)
                        second = (lambda: add_down(c - 1, 1)) if moe else None
                        if p + 1 < NP:
                            shift(p + 1, second)
                        elif moe:
                            second()
                        if moe and c < NCH:
                            hidden(FC * c + 2)
                        heads_out(p)
                        if moe and c < NCH:
                            hidden(FC * c + 3)
                    dve.wait_ge(x_dve, X.uses[:X.full(f"N{NP - 1}")].count("dve"))
                    if kind == "mla":
                        dve.wait_ge(y_used, 2 * NCH)
                        dve.tensor_tensor(acc[:, at, :], acc[:, at, :], ctxt, ALU.add).then_inc(ctx_ready, 1)
                    else:
                        dve.tensor_scalar(small[:, 1:2], small[:, 1:2], 1.0, None, ALU.mult).then_inc(ctx_ready, 1)
                        for n in range(2):
                            y = X.bank(f"Y{n}")[:, :].rearrange("p (t d) -> p t d", t=2)
                            dve.wait_ge(x_full, X.full(f"Y{n}"))
                            if kind == "spm":
                                dve.wait_ge(loaded, 32)
                                dve.tensor_tensor(qkr[:, 2 * n:2 * n + 2, 0, :], y, xb[:, 2 * n:2 * n + 2, :],
                                                  ALU.add).then_inc(h_ready, 1)
                            else:
                                dve.tensor_tensor(ctxt[:, 2 * n:2 * n + 2, :], y, xb[:, 2 * n:2 * n + 2, :],
                                                  ALU.add).then_inc(x_dve, 1)
                                dve.wait_ge(x_dve, X.uses[:X.full(f"Y{n}")].count("dve"))
                                dve.tensor_scalar(ctxt[:, 2 * n:2 * n + 2, :], ctxt[:, 2 * n:2 * n + 2, :], 100.0, -100.0,
                                                  ALU.min, ALU.max).then_inc(h_ready, 1)
                if kind == "gqa":
                    dve.wait_ge(x1_saved, 16)
                    dve.wait_ge(h_ready, 2)
                    dve.tensor_copy(acc[:, at, :], ctxt).then_inc(h_ready, 1)
                    dve.tensor_scalar(small[:, 1:2], small[:, 1:2], 1.0, None, ALU.mult).then_inc(h_ready, 1)
                    dve.wait_ge(sq_ready, 2 * NT)
                    dve.tensor_scalar(small[:, 32:36], small[:, 32:36], 1.0 / D, RMS_EPS, ALU.mult,
                                      ALU.add).then_inc(hms_ready, 1)
                    dve.wait_ge(hstd_ready, 1)
                    chain(dve.reciprocal(small[:, 28:32], small[:, 36:40]))
                    for t in range(NT):
                        dve.tensor_scalar(xb[:, t, :], ctxt[:, t, :], small[:, 28 + t:29 + t], None,
                                          ALU.mult).then_inc(hn_ready, 1)
                if routed:
                    name = "Th" if kind == "gqa" else "Tx"
                    for c in range(DC):
                        dve.wait_ge(rest_hi, c + 1)
                        dve.wait_ge(xT_ready, c + 1)
                        dve.tensor_tensor(rest_l[:, c, at_tok], xT[:, c, :], rest_h[:, c, at_tok].bitcast(F32),
                                          ALU.subtract).then_inc(x_dve, 1)
                    dve.wait_ge(x_full, X.full("R"))
                    lg = rt[:, 0, :].rearrange("p (t e) -> p t e", e=E)
                    logits = X.bank("R")[:, 0:NT * E].rearrange("p (t e) -> p t e", e=E)
                    dve.tensor_tensor(lg, logits, bcast(mem["rb"][:, :], 1, NT), ALU.add).then_inc(x_dve, 1)
                    dve.wait_ge(x_dve, X.uses[:X.full("R")].count("dve"))
                    big = mem["big"]
                    cmp = [big[:, n, :].rearrange("p (t i j) -> p t i j", t=NT, i=E) for n in range(2)]
                    other, own = bcast(lg, 2, E), bcast(lg, 3, E)
                    dve.tensor_tensor(cmp[0], other, own, ALU.is_gt).then_inc(dve_step, 1)
                    chain.n += 1
                    chain(dve.tensor_tensor(cmp[1], other, own, ALU.is_equal))
                    chain(dve.tensor_tensor(big[:, 1, :].rearrange("p (t n) -> p t n", t=NT),
                                            big[:, 1, :].rearrange("p (t n) -> p t n", t=NT),
                                            bcast(tie[:, :, :].rearrange("p i j -> p (i j)"), 1, NT), ALU.mult))
                    chain(dve.tensor_tensor(big[:, 0, :], big[:, 0, :], big[:, 1, :], ALU.add))
                    chain(dve.tensor_reduce(rt[:, 1, :], big[:, 0, :].rearrange("p (n j) -> p n j", j=E), AX.X, ALU.add))
                    chain(dve.tensor_scalar(rt[:, 2, :], rt[:, 1, :], float(routed), None, ALU.is_lt))
                    chain(dve.reduce_max(rt[:, 3, 0:NT], lg, AX.X))
                    dve.tensor_tensor(rt[:, 4, :].rearrange("p (t e) -> p t e", e=E), lg, bcast(rt[:, 3, 0:NT], 2, E),
                                      ALU.subtract).then_inc(lg_ready, 1)
                    dve.wait_ge(exp_ready, 1)
                    chain(dve.tensor_tensor(rt[:, 5, :], rt[:, 5, :], rt[:, 2, :], ALU.mult))
                    chain(dve.reduce_sum(rt[:, 3, 8:8 + NT], rt[:, 5, :].rearrange("p (t e) -> p t e", e=E), AX.X))
                    chain(dve.reciprocal(rt[:, 3, 16:16 + NT], rt[:, 3, 8:8 + NT]))
                    dve.tensor_tensor(rt[:, 6, :].rearrange("p (t e) -> p t e", e=E),
                                      rt[:, 5, :].rearrange("p (t e) -> p t e", e=E),
                                      bcast(rt[:, 3, 16:16 + NT], 2, E), ALU.mult).then_inc(comb_ready, 1)
                    dve.wait_ge(comb_ready, 1)
                    dve.tensor_scalar(combine[:, at, :], rt[:, 6, :].rearrange("p (t e) -> p t e", e=E),
                                      0.5 if kind == "none" else 1.0, None, ALU.mult).then_inc(cc_ready, 1)
                    if kind == "none":
                        for n in range(2):
                            dve.wait_ge(x_full, X.full(f"B{n}"))
                            a = acc[:, bass.ds(it * NT + 2 * n, 2), :]
                            dve.tensor_tensor(a, a, X.bank(f"B{n}")[:, :].rearrange("p (t d) -> p t d", t=2),
                                              ALU.add).then_inc(x_dve, 1)

            @block.tensor
            def _(pe):
                def take(name):
                    former = X.before(name)
                    if former:
                        pe.wait_ge(x_rel[former[0]], former[1])
                    return X.bank(name)

                def up(m):
                    c, j = m // FC, m % FC
                    for bank, full, used, first in ((gate_bank, g_full, g_used, 0), (up_bank, u_full, mem["u_rel"](u_used, a_ready), F)):
                        if m >= 1:
                            pe.wait_ge(used, m)
                        terms = [(w, x, k) for w, x in ((mem["guh"], rest_h), (mem["guh"], rest_l), (mem["gul"], rest_h))
                                 for k in range(DC)]
                        for n, (w, x, k) in enumerate(terms):
                            col = 2 * F * k + first + P * j
                            mm = pe.matmul(bank[:, :], w[:, col:col + P], x[:, k, 512 * c:512 * (c + 1)],
                                           start=(n == 0), stop=(n == len(terms) - 1))
                        mm.then_inc(full, 1)

                def down(c, half):
                    pe.wait_ge(al_ready, FC * (c + 1))
                    if c == 0:
                        pe.wait_ge(dn_split, 2)
                    if c or half:
                        pe.wait_ge(y_used, 2 * c + half)
                    for i in range(2):
                        t = 2 * half + i
                        bank = down_bank[:, D * i:D * (i + 1)]
                        terms = [(a, w, j) for a, w in ((mem["ah"], mem["dnh"]), (mem["ah"], mem["dnl"]), (mem["al"], mem["dnh"]))
                                 for j in range(FC)]
                        for n, (a, w, j) in enumerate(terms):
                            mm = pe.matmul(bank, a[:, j, P * t:P * (t + 1)], w[:, D * j:D * (j + 1)],
                                           start=(n == 0), stop=(n == len(terms) - 1))
                    mm.then_inc(y_full, 1)

                def turn(name, blocks):
                    bank = take(name)
                    for n, b in enumerate(blocks):
                        mm = pe.transpose(bank[:, P * n:P * (n + 1)], b, ident[:, :])
                    mm.then_inc(x_full, 1)

                if moe:
                    pe.wait_ge(gu_split, 4)
                    up(0)
                pe.wait_ge(xn_ready, 2 * NT if kind == "gqa" else NT)
                rows_in = ctxt if kind == "gqa" else xb
                for c in range(DC):
                    turn(f"Tx{c}", [rows_in[:, t, P * c:P * (c + 1)] for t in range(NT)])
                if moe:
                    up(1)

                def scores(which, p, u):
                    name = (which, p, u)
                    former = S.before(name)
                    if former:
                        pe.wait_ge(s_rel[former[0]], former[1])
                    bank = S.bank(name)
                    unit = (Q_UNITS if which == "q" else K_UNITS)[u]
                    for n, (j, blk, first, width) in enumerate(unit):
                        diag = first + (P * blk if which == "q" else 0)
                        pe.matmul(bank[:, diag:diag + P], ident_bf[:, :], masks_bf[:, 0 if which == "q" else 1, :],
                                  start=(n == 0), stop=False, skip_group_check=True)
                    for n, (j, blk, first, width) in enumerate(unit):
                        last = n == len(unit) - 1
                        rows_q = slice(SW * j, SW * j + (SHIFT if which == "q" else SHIFT + 2))
                        if which == "q":
                            mm = pe.matmul(bank[:, first:first + width], mem["qsT"][rows_q, P * blk:P * (blk + 1)],
                                           mem["ksT"][p % 2][rows_q, 0:width], start=False, stop=last, skip_group_check=True)
                        else:
                            mm = pe.matmul(bank[:, first:first + width], mem["ksT"][p % 2][rows_q, P * blk:P * (blk + 1)],
                                           mem["qaT"][rows_q, T - width:T], start=False, stop=last, skip_group_check=True)
                    mm.then_inc(s_full, 1)

                def counts(ring, name, who):
                    return ring.uses[:ring.full(name)].count(who)

                if attn:
                    pe.wait_ge(x_act, counts(X, "Tx1", "act"))
                    for t in range(NT):
                        tok = slice(P * t, P * (t + 1))
                        w = mem["w"]
                        if kind == "mla":
                            for c, n in enumerate("ab"):
                                bank = take(f"proj{t}{n}")
                                pe.matmul(bank[:, :], xT[:, c, tok], w[:, :, :].rearrange("p m o -> p (m o)"),
                                          start=True, stop=True).then_inc(x_full, 1)
                        else:
                            n_a = 512 if kind == "spm" else 384
                            bank = take(f"proj{t}a")
                            for c in range(DC):
                                mm = pe.matmul(bank[:, 0:n_a], xT[:, c, tok], w[:, c, 0:n_a], start=(c == 0), stop=(c == 1))
                            mm.then_inc(x_full, 1)
                            if kind == "spm":
                                bank = take(f"proj{t}b")
                                for c in range(DC):
                                    mm = pe.matmul(bank[:, 0:D], xT[:, c, tok], w[:, c, 512:768], start=(c == 0), stop=(c == 1))
                                mm.then_inc(x_full, 1)
                    if moe:
                        up(2)
                        up(3)

                    def turn_q(name, p):
                        turn(name, [mem["qst"][p % 2][:, t, :, :].rearrange("p j n -> p (j n)") for t in range(NT)])

                    def turn_k(p):
                        turn(f"Tk{p}", [mem["kst"][:, t, :, :].rearrange("p j n -> p (j n)") for t in range(NT)])

                    pe.wait_ge(stack_ready, 1)
                    turn_q("Tq0", 0)
                    turn_k(0)
                    pe.wait_ge(x_act, counts(X, "Tq0", "act"))
                    pe.wait_ge(x_dve, counts(X, "Tk0", "dve"))
                    for u in range(NU):
                        scores("q", 0, u)
                    for p in range(NP):
                        c = p + 1
                        pe.wait_ge(shift_ready, p + 1)
                        turn_q(f"Ta{p}", p)
                        if p + 1 < NP:
                            pe.wait_ge(stack_ready, p + 2)
                            turn_q(f"Tq{p + 1}", p + 1)
                            turn_k(p + 1)
                        if moe and c < NCH:
                            up(FC * c)
                        pe.wait_ge(x_act, counts(X, f"Ta{p}", "act"))
                        for u in range(NU // 2):
                            scores("k", p, u)
                        if moe:
                            down(c - 1, 0)
                        for u in range(NU // 2, NU):
                            scores("k", p, u)
                        if moe and c < NCH:
                            up(FC * c + 1)
                        if p + 1 < NP:
                            pe.wait_ge(x_act, counts(X, f"Tq{p + 1}", "act"))
                            pe.wait_ge(x_dve, counts(X, f"Tk{p + 1}", "dve"))
                            for u in range(NU // 2):
                                scores("q", p + 1, u)
                        if moe:
                            down(c - 1, 1)
                        if p + 1 < NP:
                            for u in range(NU // 2, NU):
                                scores("q", p + 1, u)
                        pe.wait_ge(s_act, counts(S, ("k", p, NU - 1), "act"))
                        bank = take(f"O{p}")
                        for kbs in ((0, 1), (3, 2)):
                            for j in range(2):
                                for half, kb in enumerate(kbs):
                                    h = 2 * p + j
                                    vh = h // (H // HKV) if kind == "gqa" else h
                                    q0 = 32 * (2 * j + half)
                                    mm = pe.matmul(bank[q0:q0 + HD + 1, P * kb:T], V[:, kb, vh, :],
                                                   mem["pt"][:, j, PT_AT[kb]:PT_AT[kb] + T - P * kb],
                                                   start=(kb < 2), stop=(kb >= 2), skip_group_check=True)
                        mm.then_inc(x_full, 1)
                        if moe and c < NCH:
                            up(FC * c + 2)
                        pe.wait_ge(x_act, counts(X, f"O{p}", "act"))
                        bank = take(f"N{p}")
                        for t in range(NT):
                            mm = pe.matmul(bank[:, 64 * t:64 * t + 34], mem["oT"][:, P * t:P * (t + 1)],
                                           halves[:, 0 if t else 1, :], start=True, stop=True)
                        mm.then_inc(x_full, 1)
                        if moe and c < NCH:
                            up(FC * c + 3)
                    if kind != "mla":
                        pe.wait_ge(ctx_ready, 1)
                        for c in range(DC):
                            turn(f"Tc{c}", [ctxt[:, t, P * c:P * (c + 1)] for t in range(NT)])
                        pe.wait_ge(x_act, counts(X, "Tc1", "act"))
                        for n in range(2):
                            bank = take(f"Y{n}")
                            for i in range(2):
                                for c in range(DC):
                                    t = 2 * n + i
                                    mm = pe.matmul(bank[:, D * i:D * (i + 1)], xT[:, c, P * t:P * (t + 1)],
                                                   mem["wo"][:, c, :], start=(c == 0), stop=(c == 1))
                            mm.then_inc(x_full, 1)
                if kind == "gqa":
                    pe.wait_ge(hn_ready, NT)
                    for c in range(DC):
                        turn(f"Th{c}", [xb[:, t, P * c:P * (c + 1)] for t in range(NT)])
                if routed:
                    pe.wait_ge(xT_ready, DC)
                    bank = take("R")
                    for t in range(NT):
                        for c in range(DC):
                            mm = pe.matmul(bank[:, E * t:E * (t + 1)], xT[:, c, P * t:P * (t + 1)], mem["wr"][:, c, :],
                                           start=(c == 0), stop=(c == 1))
                    mm.then_inc(x_full, 1)
                if kind == "none":
                    pe.wait_ge(comb_ready, 1)
                    bank = take("Cc")
                    for t in range(NT):
                        mm = pe.transpose(bank[0:E, P * t:P * (t + 1)], rt[:, 6, E * t:E * (t + 1)], ident[:, :])
                    mm.then_inc(x_full, 1)
                    pe.wait_ge(x_act, counts(X, "Cc", "act"))
                    for n in range(2):
                        bank = take(f"B{n}")
                        for i in range(2):
                            t = 2 * n + i
                            mm = pe.matmul(bank[:, D * i:D * (i + 1)], mem["cT"][:, P * t:P * (t + 1)], mem["db"][:, :],
                                           start=True, stop=True)
                        mm.then_inc(x_full, 1)
        done()

    def load(pairs, fills=()):
        new, done = sem_maker()
        loaded, filled = new("loaded"), new("filled")
        with nc.Block() as block:
            @block.sync
            def _(sp):
                for to, frm in pairs:
                    sp.dma_start(to, frm).then_inc(loaded, 16)
                sp.wait_ge(loaded, 16 * len(pairs))

            @block.vector
            def _(dve):
                for to, value in fills:
                    dve.memset(to, value).then_inc(filled, 1)
                if fills:
                    dve.wait_ge(filled, len(fills))
        done()

    def attention_buffers(st, kind):
        mem = {
            "qst": [sb(f"qst{i}", [P, NT, 2, SW], F32, st) for i in range(2)],
            "kst": sb("kst", [P, NT, 2, SW], F32, st),
            "qsT": sb("qsT", [P, T], F32R, st),
            "ksT": [sb(f"ksT{i}", [P, T], F32R, st) for i in range(2)],
            "qaT": sb("qaT", [P, T], F32R, st),
            "pt": sb("pt", [P, 2, PT_W], F32, st),
            "oT": sb("oT", [P, T], F32, st),
            "st": sb("st", [P, 8, 8], F32, st),
            "rec": sb("rec", [P, 8], F32, st),
        }
        fills = [(mem["qst"][i][:, :, :, SHIFT:SW], 0.0) for i in range(2)] + [(mem["kst"][:, :, :, SHIFT:SW], 1.0)]
        pairs = []
        if kind == "spm":
            mem["top"] = sb("top", [P, 5, 8, 8], F32, st)
            mem["keep"] = sb("keep", [P, 2, 64], F32, st)
            pairs.append((mem["keep"][:, :, :], dram["c_keep"]))
        return mem, pairs, fills

    def expert_buffers(st, mem, layer):
        mem.update({
            "layer": layer,
            "raw": sb("raw", [P, DC * 2 * F], F32, st),
            "guh": sb("guh", [P, DC * 2 * F], F32R, st),
            "gul": sb("gul", [P, DC * 2 * F], F32R, st),
            "dnh": sb("dnh", [P, FC * D], F32R, st),
            "dnl": sb("dnl", [P, FC * D], F32R, st),
            "gc": sb("gc", [P, 512], F32, st),
            "th": sb("th", [P, 512], F32, st),
            "t": [sb(f"t{i}", [P, 512], F32, st) for i in range(2)],
            "ah": sb("ah", [P, FC, 512], F32R, st),
            "al": sb("al", [P, FC, 512], F32R, st),
            "ce": sb("ce", [P, B * NT], F32, st),
            "gu_dram": dram[f"gu{layer}"],
            "dn_dram": dram[f"dn{layer}"],
            "u_rel": (lambda u_used, a_ready: u_used) if layer == 0 else (lambda u_used, a_ready: a_ready),
        })
        return [(mem["raw"][:, :], mem["gu_dram"][E - 1])]

    setup()
    with ExitStack() as st:
        mem = {"wr": sb("wr", [P, DC, E], F32, st), "rb": sb("rb", [P, E], F32, st), "db": sb("db", [E, D], F32, st),
               "cT": sb("cT", [E, T], F32, st), "big": sb("big", [P, 2, NT * E * E], F32, st)}
        load([(mem["wr"][:, :, :], dram["wr0"]), (mem["rb"][:, :], dram["rb0"]), (mem["db"][:, :], dram["db0"])])
        with nc.Fori(0, B) as it:
            iteration(it, "none", False, mem)
    with ExitStack() as st:
        mem, pairs, fills = attention_buffers(st, "mla")
        mem["w"] = sb("w_mla", [P, 4, P], F32, st)
        mem["qkn"] = sb("qkn", [P, NT * 2 * H], F32, st)
        mem["qkw"] = sb("qkw", [P, 2, HD], F32, st)
        mem["biases"] = sb("biases", [P, E, 2 * FC], F32, st)
        mem["be"] = sb("be", [P, 2 * FC], F32, st)
        pairs += expert_buffers(st, mem, 0)
        mem["sq"] = mem["oT"]
        pairs += [(mem["qkw"][:, :, :], dram["qkw"]), (mem["biases"][:, :, :], dram["gub"])]
        fold(mem["w"])
        load(pairs, fills)
        new, done = sem_maker()
        one = new("one")
        with nc.Block() as block:
            @block.vector
            def _(dve):
                dve.tensor_scalar(mem["biases"][:, :, FC:2 * FC], mem["biases"][:, :, FC:2 * FC], 1.0, None,
                                  ALU.add).then_inc(one, 1)
                dve.wait_ge(one, 1)
        done()
        with nc.Fori(0, B) as it:
            iteration(it, "mla", True, mem)
    with ExitStack() as st:
        mem, pairs, fills = attention_buffers(st, "gqa")
        mem.update({"w": sb("w_gqa", [P, DC, 384], F32, st), "wo": sb("wo_gqa", [P, DC, D], F32, st),
                    "ln": sb("ln", [P, 4], F32, st), "wr": sb("wr", [P, DC, E], F32, st), "rb": sb("rb", [P, E], F32, st),
                    "cs": sb("cs", [P, NT, 2, HD // 2], F32, st), "sq": sb("sq", [P, 512], F32, st),
                    "big": sb("big", [P, 2, NT * E * E], F32, st)})
        pairs += [(mem["w"][:, :, :], dram["w_gqa"]), (mem["wo"][:, :, :], dram["wo_gqa"]), (mem["ln"][:, :], dram["ln"]),
                  (mem["wr"][:, :, :], dram["wr1"]), (mem["cs"][:, :, :, :], dram["c_rope"])]
        fills.append((mem["rb"][:, :], 0.0))
        load(pairs, fills)
        with nc.Fori(0, B) as it:
            iteration(it, "gqa", False, mem)
    with ExitStack() as st:
        mem, pairs, fills = attention_buffers(st, "spm")
        mem.update({"w": sb("w_spm", [P, DC, 3 * D], F32, st), "wo": sb("wo_spm", [P, DC, D], F32, st)})
        pairs += [(mem["w"][:, :, :], dram["w_spm"]), (mem["wo"][:, :, :], dram["wo_spm"])]
        pairs += expert_buffers(st, mem, 1)
        load(pairs, fills)
        with nc.Fori(0, B) as it:
            iteration(it, "spm", True, mem)

    new, done = sem_maker()
    folded, reduced, turned = new("folded"), new("reduced"), new("turned")
    with nc.Block() as block:
        @block.gpsimd
        def _(pool):
            pool.partition_all_reduce(flag_all[:, :], flag[:, :], P, RMAX).then_inc(reduced, 1)

        @block.vector
        def _(dve):
            dve.wait_ge(reduced, 1)
            dve.reduce_max(flag[:, 0:1], flag_all[:, :], AX.X).then_inc(folded, 1)
            dve.wait_ge(folded, 1)
            dve.tensor_copy(flag_int[:, :], flag[:, 0:1]).then_inc(turned, 1)
            dve.wait_ge(turned, 1)
    done()
    found = nc.values_load(flag_int[0:1, 0:1], min_val=0, max_val=1)
    with nc.If(found > 0):
        nc.all_engine_barrier()
        with ExitStack() as st:
            mem, pairs, fills = attention_buffers(st, "spm")
            mem.update({"w": sb("w_gen", [P, DC, 3 * D], F32, st), "wo": sb("wo_gen", [P, DC, D], F32, st),
                        "junk": sb("junk", [P, 512], F32, st), "zero": sb("zero", [P, 512], F32, st)})
            pairs += [(mem["w"][:, :, :], dram["w_spm"]), (mem["wo"][:, :, :], dram["wo_spm"])]
            fills.append((mem["zero"][:, :], 0.0))
            load(pairs, fills)
            with nc.Fori(0, B) as it:
                iteration(it, "spm", False, mem, general=True)
        nc.all_engine_barrier()
    nc.end_ifs()

    with nc.Fori(0, B) as it:
        new, done = sem_maker()
        loaded, clipped, summed, stored = new("loaded"), new("clipped"), new("summed"), new("stored")
        at = bass.ds(it * NT, NT)
        with nc.Block() as block:
            @block.sync
            def _(sp):
                sp.dma_start(xb[:, :, :], z_rows[it]).then_inc(loaded, 16)
                sp.wait_ge(loaded, 16)
                sp.wait_ge(summed, 1)
                sp.dma_start(out_rows[it], xb[:, :, :]).then_inc(stored, 16)
                sp.wait_ge(stored, 16)

            @block.vector
            def _(dve):
                dve.tensor_scalar(qkr[:, :, 0, :], acc[:, at, :], 100.0, -100.0, ALU.min, ALU.max).then_inc(clipped, 1)
                dve.wait_ge(clipped, 1)
                dve.wait_ge(loaded, 16)
                dve.tensor_tensor(xb[:, :, :], xb[:, :, :], qkr[:, :, 0, :], ALU.add).then_inc(summed, 1)
        done()


def kernel(**inputs):
    import concourse.bacc as bacc
    from concourse.bass_utils import run_bass_kernel_spmd

    a = {k: np.asarray(v) for k, v in inputs.items()}

    def chunks(w):
        return np.ascontiguousarray(w.reshape(-1, P, w.shape[-1]).transpose(1, 0, 2))

    def experts(w):
        return np.ascontiguousarray(w.reshape(E, -1, P, w.shape[-1]).transpose(0, 2, 1, 3).reshape(E, P, -1))

    def everywhere(v):
        return np.ascontiguousarray(np.broadcast_to(v, (P,) + v.shape))

    f4 = np.float32
    rows = np.arange(P)
    mask = np.where(rows[None, :] > rows[:, None], f4(MASKED), f4(0))
    halves = np.zeros((P, 2, 34), f4)
    for j in range(2):
        for d in range(HD + 1):
            halves[64 * j + d, :, (HD + 1) * j + d] = 1
            halves[64 * j + 32 + d, 0, (HD + 1) * j + d] = 1
    freqs = np.arange(T, dtype=f4)[:, None] * (f4(1) / f4(10000.0) ** (np.arange(0, HD, 2, dtype=f4) / f4(HD)))
    rope = np.stack([np.cos(freqs), np.sin(freqs)], 1).astype(f4)
    data = {
        "x": a["L0_attn_x"].reshape(NTOK, D),
        "c_ident": np.eye(P, dtype=f4),
        "c_masks": np.stack([mask, mask.T], 1),
        "c_halves": halves,
        "c_tie": everywhere(np.tril(np.ones((E, E), f4), -1)),
        "c_block": (rows[:, None] // HD == np.arange(8)[None, :]).astype(f4),
        "c_keep": everywhere(np.stack([np.tile(np.r_[f4(0), np.ones(7, f4)], 8), np.tile(np.arange(1, 9, dtype=f4), 8)])),
        "c_rope": np.ascontiguousarray(rope.reshape(NT, P, 2, HD // 2).transpose(1, 0, 2, 3)),
        "dq": np.tile(a["L0_attn_W_DQ"], (1, 8)),
        "uq": a["L0_attn_W_UQ"].T,
        "dkv": chunks(np.tile(a["L0_attn_W_DKV"], (1, 8))),
        "ukv": chunks(a["L0_attn_W_UKV"].T),
        "kr": np.tile(a["L0_attn_W_KR"], (1, 8)),
        "qr": a["L0_attn_W_QR"],
        "wo": a["L0_attn_W_O"].T,
        "qkw": everywhere(np.stack([a["L0_attn_q_norm_w"], a["L0_attn_k_norm_w"]])),
        "wr0": chunks(a["L0_ffn_router_weight"].T),
        "rb0": everywhere(a["L0_ffn_router_bias"]),
        "gub": a["L0_ffn_gate_up_proj_bias"].reshape(E, 2 * FC, P).transpose(2, 0, 1),
        "db0": a["L0_ffn_down_proj_bias"],
        "gu0": np.roll(experts(a["L0_ffn_gate_up_proj"].transpose(0, 2, 1)), -1, axis=0),
        "dn0": experts(a["L0_ffn_down_proj"].transpose(0, 2, 1)),
        "w_gqa": chunks(np.concatenate([a["L1_ffn_Wq"], a["L1_ffn_Wk"], a["L1_ffn_Wv"]], 1)),
        "wo_gqa": chunks(a["L1_ffn_Wo"]),
        "ln": np.concatenate([a["L1_ffn_ln1_w"].reshape(DC, P).T, a["L1_ffn_ln2_w"].reshape(DC, P).T], 1),
        "wr1": chunks(a["L1_ffn_Wr"]),
        "gu1": np.roll(experts(np.concatenate([a["L1_ffn_Wg"], a["L1_ffn_Wu"]], 2)), -1, axis=0),
        "dn1": experts(a["L1_ffn_Wd"]),
        "w_spm": chunks(np.concatenate([a["L1_attn_Wq"].T, a["L1_attn_Wk"].T, a["L1_attn_Wv"].T], 1)),
        "wo_spm": chunks(a["L1_attn_Wo"].T),
    }
    nc = bacc.Bacc("TRN2", target_bir_lowering=False, num_devices=1, dynamic_dma_scratch_size=1024)
    data = {f"in_{k}": np.ascontiguousarray(v) for k, v in data.items()}
    dram = {k[3:]: nc.dram_tensor(k, list(v.shape), mybir.dt.from_np(v.dtype), kind="ExternalInput").ap()
            for k, v in data.items()}
    outs = {"out": nc.dram_tensor("out", [NTOK, D], F32, kind="ExternalOutput").ap()}
    program(nc, dram, outs)
    r = run_bass_kernel_spmd(nc, [data], core_ids=[0])
    return r.results[0]["out"].reshape(B, T, D)
```

```python
from contextlib import ExitStack

import numpy as np

import concourse.bass as bass
from concourse import mybir

P = 128
F32 = mybir.dt.float32
F32R = mybir.dt.float32r
BF16 = mybir.dt.bfloat16
I32 = mybir.dt.int32
ALU = mybir.AluOpType
ACT = mybir.ActivationFunctionType
AX = mybir.AxisListType
RMAX = bass.bass_isa.ReduceOp.max

B, T, D = 8, 512, 256
H, HD = 16, 16
HKV = 4
E, F = 8, 512
NT = T // P
DC = D // P
FC = F // P
NP = H // 2
NTOK = B * T
NCH = NTOK // 512
SW = 64
SHIFT = 3 * HD
MASKED = -1.0e30
LN_EPS, QK_EPS, RMS_EPS = 1e-5, 1.1920929e-07, 1e-5
ALPHA, LIMIT = 1.702, 7.0
NEWTON = 21

Q_UNITS = []
K_UNITS = []
for _j in range(2):
    Q_UNITS += [[(_j, 3, 0, 512)], [(_j, 2, 0, 384), (_j, 0, 384, 128)], [(_j, 1, 0, 256)]]
    K_UNITS += [[(_j, 0, 0, 512)], [(_j, 3, 0, 128), (_j, 1, 128, 384)], [(_j, 2, 0, 256)]]
NU = len(Q_UNITS)
PT_AT = {0: 0, 3: 512, 1: 640, 2: 1024}
PT_W = 1280


class Chain:

    def __init__(self, eng, sem):
        self.eng, self.sem, self.n = eng, sem, 0

    def __call__(self, ins):
        self.n += 1
        ins.then_inc(self.sem, 1)
        self.eng.wait_ge(self.sem, self.n)


class Ring:

    def __init__(self, banks):
        self.banks, self.uses, self.at = banks, [], {}

    def add(self, name, engine):
        self.at[name] = len(self.uses)
        self.uses.append(engine)

    def bank(self, name):
        return self.banks[self.at[name] % len(self.banks)]

    def full(self, name):
        return self.at[name] + 1

    def before(self, name):
        n = self.at[name] - len(self.banks)
        if n < 0:
            return None
        return self.uses[n], self.uses[:n + 1].count(self.uses[n])


def bcast(ap, axis, n):
    shape = list(ap.shape)
    shape.insert(axis, n)
    return ap.unsqueeze(axis).broadcast_to(shape)


def program(nc, dram, outs):
    ctx = ExitStack()
    with ctx:
        build(nc, dram, outs, ctx)


def build(nc, dram, outs, ctx):
    def sb(name, shape, dt=F32, stack=ctx):
        if stack is not ctx:
            name = f"{name}_{nc.next_id()}"
        return stack.enter_context(nc.sbuf_tensor(name, shape, dt))

    out = outs["out"]
    x_rows = dram["x"].rearrange("(b t p) d -> b p t d", p=P, t=NT)
    out_rows = out.rearrange("(b t p) d -> b p t d", p=P, t=NT)
    x1_dram = nc.dram_tensor("x1_scratch", [NTOK + T, D], F32).ap()
    z_dram = nc.dram_tensor("z_scratch", [NTOK, D], F32).ap()
    x1_rows = x1_dram.rearrange("(b t p) d -> b p t d", p=P, t=NT)
    z_rows = z_dram.rearrange("(b t p) d -> b p t d", p=P, t=NT)

    banks = [ctx.enter_context(nc.psum_tensor(f"bank{i}", [P, 512], F32)) for i in range(8)]
    x_banks, gate_bank, up_bank, down_bank = banks[0:2], banks[2], banks[3], banks[4]

    ident = sb("ident", [P, P])
    ident_bf = sb("ident_bf", [P, P], BF16)
    masks_bf = sb("masks_bf", [P, 2, 2, P], BF16)
    tie = sb("tie", [P, E, E])
    flag = sb("flag", [P, 8])
    minus_half = sb("minus_half", [P, NT])
    flag_all = sb("flag_all", [P, 8])
    flag_int = sb("flag_int", [P, 1], I32)
    combine = sb("combine", [P, B * NT, E])
    acc = sb("acc", [P, B * NT, D])
    rest_h = sb("rest_h", [P, DC, NTOK], F32R)
    rest_l = sb("rest_l", [P, DC, NTOK], F32R)
    V = sb("V", [P, NT, H, HD + 1])
    xb = sb("xb", [P, NT, D])
    xT = sb("xT", [P, DC, T])
    qkr = sb("qkr", [P, NT, 3, D])
    small = sb("small", [P, 64])
    rt = sb("rt", [P, 8, NT * E])

    def sem_maker():
        made = []

        def new(name):
            s = nc.alloc_semaphore(f"{name}_{nc.next_id()}")
            made.append(s)
            return s

        def done():
            nc.clear_and_free_semaphores(made)
            nc.all_engine_barrier()
        return new, done

    def setup():
        new, done = sem_maker()
        with ExitStack() as st:
            masks = sb("masks", [P, 2, P], F32, st)
            loaded, cast, filled = new("loaded"), new("cast"), new("filled")
            with nc.Block() as block:
                @block.sync
                def _(sp):
                    sp.dma_start(ident[:, :], dram["c_ident"]).then_inc(loaded, 16)
                    sp.dma_start(masks[:, :, :], dram["c_masks"]).then_inc(loaded, 16)
                    sp.dma_start(tie[:, :, :], dram["c_tie"]).then_inc(loaded, 16)
                    for b in range(B):
                        sp.dma_start(acc[:, NT * b:NT * (b + 1), :], x_rows[b]).then_inc(loaded, 16)
                    sp.wait_ge(loaded, 16 * (3 + B))

                @block.vector
                def _(dve):
                    dve.memset(V[:, :, :, HD:HD + 1], 1.0).then_inc(filled, 1)
                    dve.memset(flag[:, :], 0.0).then_inc(filled, 1)
                    dve.memset(minus_half[:, :], -0.5).then_inc(filled, 1)
                    dve.wait_ge(loaded, 16 * (3 + B))
                    dve.tensor_copy(ident_bf[:, :], ident[:, :]).then_inc(cast, 1)
                    dve.tensor_copy(masks_bf[:, :, :, :], bcast(masks[:, :, :], 2, 2)).then_inc(cast, 1)
                    dve.wait_ge(cast, 2)
                    dve.wait_ge(filled, 3)
            done()

    def fold(weights):
        new, done = sem_maker()
        with ExitStack() as st:
            dq = sb("f_dq", [P, P], F32, st)
            uq = sb("f_uq", [P, HD], F32, st)
            dkv = sb("f_dkv", [P, 2, P], F32, st)
            ukv = sb("f_ukv", [P, 2, 2 * HD], F32, st)
            kr = sb("f_kr", [64, P], F32, st)
            qr = sb("f_qr", [64, HD], F32, st)
            wo = sb("f_wo", [HD, HD], F32, st)
            av = sb("f_av", [HD, P], F32, st)
            four = sb("f_four", [P, 4, HD], F32, st)
            bm = sb("f_bm", [P, 8], F32, st)
            loaded, products, copied, value = new("loaded"), new("products"), new("copied"), new("value")
            ps, pv = banks[0], banks[1]
            with nc.Block() as block:
                @block.sync
                def _(sp):
                    for to, name in ((dq, "dq"), (uq, "uq"), (dkv, "dkv"), (ukv, "ukv"), (kr, "kr"),
                                     (qr, "qr"), (wo, "wo"), (bm, "c_block")):
                        sp.dma_start(to[tuple(slice(None) for _ in to.shape)], dram[name]).then_inc(loaded, 16)

                @block.tensor
                def _(pe):
                    pe.wait_ge(loaded, 16 * 8)
                    pe.matmul(ps[:, 0:16], dq[:, :], uq[:, :], start=True, stop=True)
                    for c in range(2):
                        pe.matmul(ps[:, 16:32], dkv[:, c, :], ukv[:, c, 0:HD], start=(c == 0), stop=(c == 1))
                    pe.matmul(ps[:, 32:48], kr[:, :], qr[:, :], start=True, stop=True)
                    for c in range(2):
                        mm = pe.matmul(pv[0:HD, 0:P], ukv[:, c, HD:2 * HD], dkv[:, c, :],
                                       start=(c == 0), stop=(c == 1))
                    mm.then_inc(products, 1)
                    pe.wait_ge(value, 1)
                    pe.matmul(ps[:, 48:64], av[:, :], wo[:, :], start=True, stop=True).then_inc(products, 1)

                @block.vector
                def _(dve):
                    dve.wait_ge(products, 1)
                    dve.tensor_copy(av[:, :], pv[0:HD, 0:P]).then_inc(value, 1)
                    dve.wait_ge(products, 2)
                    dve.tensor_copy(four[:, :, :], ps[:, 0:64].rearrange("p (m o) -> p m o", m=4)).then_inc(copied, 1)
                    dve.wait_ge(copied, 1)
                    for m in range(4):
                        dve.tensor_tensor(weights[:, m, :].rearrange("p (h o) -> p h o", o=HD),
                                          bcast(four[:, m, :], 1, 8), bcast(bm[:, :], 2, HD),
                                          ALU.mult).then_inc(copied, 1)
                    dve.wait_ge(copied, 5)
            done()

    def split_high(mem, act, gu_high):
        for q in range(4):
            act.activation(mem["guh"][:, 512 * q:512 * (q + 1)], mem["raw"][:, 512 * q:512 * (q + 1)],
                           ACT.Copy).then_inc(gu_high, 1)

    def split_low(mem, dve, gu_high, gu_split):
        for q in range(4):
            dve.wait_ge(gu_high, q + 1)
            sl = slice(512 * q, 512 * (q + 1))
            dve.tensor_tensor(mem["gul"][:, sl], mem["raw"][:, sl], mem["guh"][:, sl].bitcast(F32),
                              ALU.subtract).then_inc(gu_split, 1)

    def split_first(mem):
        new, done = sem_maker()
        gu_high, gu_split = new("gu_high"), new("gu_split")
        with nc.Block() as block:
            @block.scalar
            def _(act):
                split_high(mem, act, gu_high)

            @block.vector
            def _(dve):
                split_low(mem, dve, gu_high, gu_split)
        done()

    def iteration(it, kind, moe, mem, general=False, z_stored=None):
        new, done = sem_maker()
        attn = kind in ("mla", "gqa", "spm")
        routed = {"none": 4, "gqa": 2}.get(kind, 0)
        s_banks = banks[5:8] if moe else banks[2:8]
        at = bass.ds(it * NT, NT)
        at_tok = bass.ds(it * T, T)

        late = 0 if moe else 1
        X = Ring(x_banks)
        X.add("Tx0", "act")
        X.add("Tx1", "act")
        if attn:
            for t in range(NT):
                X.add(f"proj{t}a", "act")
                if kind != "gqa":
                    X.add(f"proj{t}b", "act")
            X.add("Tq0", "act")
            X.add("Tk0", "dve")
            for p in range(NP + late):
                if moe:
                    X.add(f"Ta{p}", "act")
                if p + 1 < NP:
                    X.add(f"Tq{p + 1}", "act")
                    X.add(f"Tk{p + 1}", "dve")
                if not moe and p < NP:
                    X.add(f"Ta{p}", "act")
                if p >= late:
                    X.add(f"O{p - late}", "act")
                    X.add(f"N{p - late}", "dve")
            if kind != "mla":
                for n, who in (("Tc0", "act"), ("Tc1", "act"), ("Y0", "dve"), ("Y1", "dve")):
                    X.add(n, who)
        if kind == "gqa":
            X.add("Th0", "dve")
            X.add("Th1", "dve")
        if kind == "none":
            X.uses[0] = X.uses[1] = "dve"
        if routed:
            X.add("R", "dve")
        if kind == "none":
            for n, who in (("Cc", "act"), ("B0", "dve"), ("B1", "dve")):
                X.add(n, who)
        S = Ring(s_banks)
        if attn:
            for u in range(NU):
                S.add(("q", 0, u), "dve")
            for p in range(NP):
                if moe:
                    for u in range(NU):
                        S.add(("k", p, u), "act")
                if p + 1 < NP:
                    for u in range(NU):
                        S.add(("q", p + 1, u), "dve")
                if not moe:
                    for u in range(NU):
                        S.add(("k", p, u), "act")

        x_full, x_act, x_dve = new("x_full"), new("x_act"), new("x_dve")
        s_full, s_act, s_dve = new("s_full"), new("s_act"), new("s_dve")
        x_rel = {"act": x_act, "dve": x_dve}
        s_rel = {"act": s_act, "dve": s_dve}
        dve_step, pool_step = new("dve_step"), new("pool_step")
        loaded, next_rows, x1_saved = new("loaded"), new("next_rows"), new("x1_saved")
        var_ready, std_ready, xn_ready = new("var_ready"), new("std_ready"), new("xn_ready")
        ms_ready, rms_ready = new("ms_ready"), new("rms_ready")
        sq_ready, xT_ready = new("sq_ready"), new("xT_ready")
        proj_ready, qk_ready = new("proj_ready"), new("qk_ready")
        qk_ms, qk_std = new("qk_ms"), new("qk_std")
        stack_ready, shift_ready, ctx_ready = new("stack_ready"), new("shift_ready"), new("ctx_ready")
        h_ready, hms_ready, hstd_ready, hn_ready = (
            new("h_ready"), new("hms_ready"), new("hstd_ready"), new("hn_ready"))
        rest_hi, lg_ready, exp_ready, comb_ready, cc_ready = (
            new("rest_hi"), new("lg_ready"), new("exp_ready"), new("comb_ready"), new("cc_ready"))
        if moe:
            gu_high, gu_split, dn_loaded, dn_high, dn_split, gu_next = (
                new("gu_high"), new("gu_split"), new("dn_loaded"), new("dn_high"), new("dn_split"), new("gu_next"))
            g_full, g_used, u_full, u_used = new("g_full"), new("g_used"), new("u_full"), new("u_used")
            th_ready, a_ready, ah_ready, al_ready = new("th_ready"), new("a_ready"), new("ah_ready"), new("al_ready")
            y_full, y_used, picked = new("y_full"), new("y_used"), new("picked")

        ctxt = qkr[:, :, 2, :]

        block = nc.Block()
        with block as block:
            @block.sync
            def _(sp):
                if kind == "gqa":
                    sp.dma_start(x1_rows[it], acc[:, at, :]).then_inc(x1_saved, 16)
                if moe:
                    sp.dma_start(mem["raw"][:, 0:FC * D], mem["dn_dram"][it]).then_inc(dn_loaded, 16)
                    sp.wait_ge(dn_split, 2)
                    sp.dma_start(mem["raw"][:, :], mem["gu_dram"][it]).then_inc(gu_next, 16)
                if kind in ("mla", "spm"):
                    sp.wait_ge(x_full, X.full("Tx1"))
                    sp.dma_start(xb[:, :, :], (x_rows if kind == "mla" else x1_rows)[it + 1]).then_inc(next_rows, 16)
                if kind == "spm":
                    sp.wait_ge(stack_ready, NP)
                    sp.dma_start(qkr[:, :, 1, :], x1_rows[it]).then_inc(loaded, 16)
                    sp.wait_ge(h_ready, 2)
                    sp.dma_start(z_rows[it], qkr[:, :, 0, :]).then_inc(z_stored, 16)
                if kind in ("mla", "spm"):
                    sp.wait_ge(next_rows, 16)
                if kind == "gqa":
                    sp.wait_ge(x1_saved, 16)
                if moe:
                    sp.wait_ge(gu_next, 16)

            @block.gpsimd
            def _(pool):
                chain = Chain(pool, pool_step)

                def low(m):
                    j = m % FC
                    pool.wait_ge(ah_ready, m + 1)
                    pool.tensor_tensor(mem["al"][:, j, :], mem["t"][m % 2][:, :], mem["ah"][:, j, :].bitcast(F32),
                                       ALU.subtract).then_inc(al_ready, 1)

                def stack(p):
                    if p == 0:
                        pool.wait_ge(qk_ready, {"mla": 1, "gqa": 2 * (NT + 1), "spm": 1}[kind])
                    if p == 2 and kind == "mla":
                        pool.wait_ge(qk_ready, 2)
                    if p >= 1:
                        pool.wait_ge(x_full, X.full(f"Tk{p - 1}"))
                    if p >= 2:
                        pool.wait_ge(x_full, X.full(f"Ta{p - 2}"))
                    qs, ks = mem["qst"][p % 2], mem["kst"]
                    q = qkr[:, :, 0, 2 * HD * p:2 * HD * (p + 1)].rearrange("p t (j d) -> p t j d", j=2)
                    if kind == "gqa":
                        g = p // (NP // HKV)
                        k = bcast(qkr[:, :, 1, HD * g:HD * (g + 1)], 2, 2)
                    else:
                        k = qkr[:, :, 1, 2 * HD * p:2 * HD * (p + 1)].rearrange("p t (j d) -> p t j d", j=2)
                    pool.tensor_copy(qs[:, :, :, 0:HD].bitcast(F32R), q).then_inc(pool_step, 1)
                    pool.tensor_copy(ks[:, :, :, 0:HD].bitcast(F32R), k).then_inc(pool_step, 1)
                    chain.n += 2
                    pool.wait_ge(pool_step, chain.n)
                    pool.tensor_tensor(qs[:, :, :, HD:2 * HD], q, qs[:, :, :, 0:HD], ALU.subtract).then_inc(pool_step, 1)
                    pool.tensor_tensor(ks[:, :, :, 2 * HD:3 * HD], k, ks[:, :, :, 0:HD], ALU.subtract).then_inc(pool_step, 1)
                    pool.tensor_copy(qs[:, :, :, 2 * HD:3 * HD], qs[:, :, :, 0:HD]).then_inc(pool_step, 1)
                    chain.n += 3
                    pool.wait_ge(pool_step, chain.n)
                    pool.tensor_copy(ks[:, :, :, HD:2 * HD], ks[:, :, :, 0:HD]).then_inc(stack_ready, 1)

                def rsqrt(to, frm, ready, done_sem):
                    pool.wait_ge(*ready)
                    pool.tensor_tensor(to, frm, minus_half[:, 0:frm.shape[-1]], ALU.pow).then_inc(done_sem, 1)

                rsqrt(small[:, 4:8], small[:, 0:4], (var_ready, 1), std_ready)
                if kind == "gqa":
                    rsqrt(small[:, 20:24], small[:, 16:20], (ms_ready, 1), rms_ready)
                if attn:
                    if moe:
                        low(0)
                    stack(0)
                    if moe:
                        low(1)
                        low(2)
                    stack(1)
                    for p in range(NP):
                        c = p + 1
                        if moe:
                            low(FC * c - 1)
                        if p + 2 < NP:
                            stack(p + 2)
                        if moe and c < NCH:
                            for j in range(FC - 1):
                                low(FC * c + j)
                if kind == "gqa":
                    pool.wait_ge(x1_saved, 16)
                    pool.wait_ge(h_ready, 2)
                    rsqrt(small[:, 28:32], small[:, 36:40], (hms_ready, 1), hstd_ready)
                    pool.tensor_copy(acc[:, at, :], ctxt).then_inc(pool_step, 1)

            @block.scalar
            def _(act):

                def gate(m):
                    if mem["layer"] == 0:
                        act.wait_ge(g_used, m + 1)
                        if m >= 1:
                            act.wait_ge(a_ready, m)
                        act.activation(mem["th"][:, :], mem["gc"][:, :], ACT.Tanh,
                                       scale=ALPHA / 2).then_inc(th_ready, 1)
                    else:
                        act.wait_ge(g_full, m + 1)
                        if m >= 2:
                            act.wait_ge(a_ready, m - 1)
                        act.activation((mem["gc"], mem["th"])[m % 2][:, :], gate_bank[:, :],
                                       ACT.Silu).then_inc(g_used, 1)

                def high(m):
                    act.wait_ge(a_ready, m + 1)
                    if m >= FC:
                        act.wait_ge(y_full, 2 * (m // FC))
                    act.activation(mem["ah"][:, m % FC, :], mem["t"][m % 2][:, :], ACT.Copy).then_inc(ah_ready, 1)

                def down_high():
                    act.wait_ge(dn_loaded, 16)
                    for q in range(2):
                        act.activation(mem["dnh"][:, 512 * q:512 * (q + 1)], mem["raw"][:, 512 * q:512 * (q + 1)],
                                       ACT.Copy).then_inc(dn_high, 1)

                if moe:
                    gate(0)
                for c in range(DC):
                    act.wait_ge(x_full, X.full(f"Tx{c}"))
                    if kind == "gqa":
                        act.activation(xT[:, c, :], X.bank(f"Tx{c}")[:, :], ACT.Copy,
                                       scale=mem["ln"][:, c:c + 1]).then_inc(x_act, 1)
                    elif kind == "none":
                        act.activation(xT[:, c, :], X.bank(f"Tx{c}")[:, :], ACT.Copy).then_inc(xT_ready, 1)
                        act.activation(rest_h[:, c, at_tok], X.bank(f"Tx{c}")[:, :], ACT.Copy).then_inc(rest_hi, 1)
                    else:
                        act.activation(xT[:, c, :], X.bank(f"Tx{c}")[:, :], ACT.Copy).then_inc(x_act, 1)
                if moe:
                    down_high()
                    high(0)
                    gate(1)
                if attn:
                    scale = 1.0 / 4.0
                    for t in range(NT):
                        act.wait_ge(x_full, X.full(f"proj{t}a"))
                        a = X.bank(f"proj{t}a")
                        if kind == "mla":
                            for c, n in enumerate("ab"):
                                a = X.bank(f"proj{t}{n}")
                                act.wait_ge(x_full, X.full(f"proj{t}{n}"))
                                act.activation(qkr[:, t, :, P * c:P * (c + 1)],
                                               a[:, 0:3 * P].rearrange("p (m o) -> p m o", m=3), ACT.Copy).then_inc(proj_ready, 1)
                                act.activation(V[:, t, 8 * c:8 * (c + 1), 0:HD],
                                               a[:, 3 * P:4 * P].rearrange("p (h o) -> p h o", o=HD), ACT.Copy).then_inc(x_act, 1)
                        elif kind == "spm":
                            if t == 0:
                                act.wait_ge(z_stored, (it + 1) * 16)
                            act.activation(qkr[:, t, 0, :], a[:, 0:D], ACT.Copy, scale=scale).then_inc(proj_ready, 1)
                            act.activation(qkr[:, t, 1, :], a[:, D:2 * D], ACT.Copy).then_inc(x_act, 1)
                            v = X.bank(f"proj{t}b")
                            act.wait_ge(x_full, X.full(f"proj{t}b"))
                            act.activation(V[:, t, :, 0:HD], v[:, 0:D].rearrange("p (h o) -> p h o", o=HD),
                                           ACT.Copy).then_inc(x_act, 1)
                        else:
                            act.activation(qkr[:, t, 0, :], a[:, 0:D], ACT.Copy, scale=scale).then_inc(proj_ready, 1)
                            act.activation(qkr[:, t, 1, 0:64], a[:, D:D + 64], ACT.Copy).then_inc(proj_ready, 1)
                            act.activation(V[:, t, 0:HKV, 0:HD],
                                           a[:, D + 64:D + 128].rearrange("p (h o) -> p h o", o=HD),
                                           ACT.Copy).then_inc(x_act, 1)
                    if kind == "mla":
                        act.wait_ge(qk_ms, 2)
                        act.activation(mem["qkn"][:, :], mem["qkn"][:, :], ACT.Sqrt).then_inc(qk_std, 1)
                    if moe:
                        high(1)
                        gate(2)
                        high(2)
                        gate(3)

                    def take_q(p):
                        act.wait_ge(x_full, X.full(f"Tq{p}"))
                        act.activation(mem["qsT"][:, :], X.bank(f"Tq{p}")[:, :], ACT.Copy).then_inc(x_act, 1)

                    def probabilities(p):
                        if p >= 1:
                            act.wait_ge(x_full, X.full(f"O{p - 1}"))
                        for u in range(NU):
                            unit, bank = K_UNITS[u], S.bank(("k", p, u))
                            act.wait_ge(s_full, S.full(("k", p, u)))
                            j, first = unit[0][0], PT_AT[unit[0][1]]
                            width = sum(w for _, _, _, w in unit)
                            to, frm = mem["pt"][:, j, first:first + width], bank[:, 0:width]
                            act.activation(to, frm, ACT.Relu if kind == "spm" else ACT.Exp).then_inc(s_act, 1)

                    def take_qa(p):
                        act.wait_ge(x_full, X.full(f"Ta{p}"))
                        act.activation(mem["qaT"][:, :], X.bank(f"Ta{p}")[:, :], ACT.Copy).then_inc(x_act, 1)

                    def take_o(p):
                        act.wait_ge(x_full, X.full(f"O{p}"))
                        act.activation(mem["oT"][:, :], X.bank(f"O{p}")[:, :], ACT.Copy).then_inc(x_act, 1)

                    take_q(0)
                    if not moe:
                        for p in range(NP + late):
                            if p + 1 < NP:
                                take_q(p + 1)
                            if p < NP:
                                take_qa(p)
                            if p >= 1:
                                take_o(p - 1)
                            if p < NP:
                                probabilities(p)
                    for p in range(NP if moe else 0):
                        c = p + 1
                        take_qa(p)
                        if p + 1 < NP:
                            take_q(p + 1)
                        if moe:
                            high(FC * c - 1)
                        if moe and c < NCH:
                            gate(FC * c)
                        probabilities(p)
                        if moe and c == NCH:
                            act.wait_ge(gu_next, 16)
                            act.wait_ge(u_full, NCH * FC)
                            split_high(mem, act, gu_high)
                        if moe and c < NCH:
                            gate(FC * c + 1)
                            high(FC * c)
                            high(FC * c + 1)
                        take_o(p)
                        if moe and c < NCH:
                            gate(FC * c + 2)
                            high(FC * c + 2)
                            gate(FC * c + 3)
                    if kind != "mla":
                        for c in range(DC):
                            act.wait_ge(x_full, X.full(f"Tc{c}"))
                            act.activation(xT[:, c, :], X.bank(f"Tc{c}")[:, :], ACT.Copy).then_inc(x_act, 1)
                if kind == "gqa":
                    for t in range(NT):
                        act.wait_ge(h_ready, t // 2 + 1)
                        act.activation(qkr[:, t, 0, :], ctxt[:, t, :], ACT.Square,
                                       accum_out=small[:, 32 + t:33 + t]).then_inc(sq_ready, 1)
                    for c in range(DC):
                        act.wait_ge(x_full, X.full(f"Th{c}"))
                        act.activation(xT[:, c, :], X.bank(f"Th{c}")[:, :], ACT.Copy,
                                       scale=mem["ln"][:, 2 + c:3 + c]).then_inc(xT_ready, 1)
                        act.wait_ge(xT_ready, c + 1)
                        act.activation(rest_h[:, c, at_tok], xT[:, c, :], ACT.Copy).then_inc(rest_hi, 1)
                if routed:
                    act.wait_ge(lg_ready, 1)
                    act.activation(rt[:, 5, :], rt[:, 4, :], ACT.Exp).then_inc(exp_ready, 1)
                if kind == "none":
                    act.wait_ge(x_full, X.full("Cc"))
                    act.activation(mem["cT"][:, :], X.bank("Cc")[0:E, :], ACT.Copy).then_inc(x_act, 1)

            @block.vector
            def _(dve):
                chain = Chain(dve, dve_step)
                if moe:
                    dve.tensor_copy(mem["ce"][:, :], combine[:, :, bass.ds(it, 1)]).then_inc(picked, 1)
                    if mem["layer"] == 0:
                        dve.tensor_copy(mem["be"][:, :], mem["biases"][:, bass.ds(it, 1), :]).then_inc(picked, 1)
                if kind in ("mla", "spm"):
                    src = [xb[:, t, :] for t in range(NT)]
                else:
                    src = [acc[:, bass.ds(it * NT + t, 1), :] for t in range(NT)]
                for t in range(NT):
                    dve.bn_stats(small[:, 40 + 6 * t:46 + 6 * t], src[t]).then_inc(dve_step, 1)
                chain.n += NT
                dve.wait_ge(dve_step, chain.n)
                for t in range(NT):
                    dve.bn_aggr(small[:, 8 + 2 * t:10 + 2 * t], small[:, 40 + 6 * t:46 + 6 * t]).then_inc(dve_step, 1)
                chain.n += NT
                dve.wait_ge(dve_step, chain.n)
                mean_var = small[:, 8:16].rearrange("p (t two) -> p t two", two=2)
                dve.tensor_scalar(small[:, 0:4], mean_var[:, :, 1], LN_EPS, None, ALU.add).then_inc(var_ready, 1)
                dve.wait_ge(std_ready, 1)
                if kind == "gqa":
                    chain(dve.tensor_tensor(small[:, 16:20], small[:, 4:8], small[:, 4:8], ALU.mult))
                    chain(dve.tensor_tensor(small[:, 16:20], small[:, 16:20], mean_var[:, :, 1], ALU.mult))
                    dve.tensor_scalar(small[:, 16:20], small[:, 16:20], RMS_EPS, None, ALU.add).then_inc(ms_ready, 1)
                    dve.wait_ge(rms_ready, 1)
                    chain(dve.tensor_tensor(small[:, 24:28], small[:, 20:24], small[:, 4:8], ALU.mult))
                    for t in range(NT):
                        dve.tensor_scalar(ctxt[:, t, :], src[t], small[:, 8 + 2 * t:9 + 2 * t], small[:, 24 + t:25 + t],
                                          ALU.subtract, ALU.mult).then_inc(xn_ready, 1)
                for t in range(NT):
                    dve.tensor_scalar(xb[:, t, :], src[t], small[:, 8 + 2 * t:9 + 2 * t], small[:, 4 + t:5 + t],
                                      ALU.subtract, ALU.mult).then_inc(xn_ready, 1)

                def hidden(m):
                    clip(m)
                    multiply(m)

                def clip(m):
                    j = m % FC
                    t = mem["t"][m % 2]
                    if m == 0 and mem["layer"] == 0:
                        dve.wait_ge(picked, 2)
                    if mem["layer"] == 0:
                        dve.wait_ge(g_full, m + 1)
                        if m >= 1:
                            dve.wait_ge(a_ready, m)
                        dve.tensor_scalar(mem["gc"][:, :], gate_bank[:, :], mem["be"][:, j:j + 1], LIMIT,
                                          ALU.add, ALU.min).then_inc(g_used, 1)
                    dve.wait_ge(u_full, m + 1)
                    if m >= 2:
                        dve.wait_ge(al_ready, m - 1)
                    if mem["layer"] == 0:
                        dve.tensor_scalar(t[:, :], up_bank[:, :], mem["be"][:, FC + j:FC + j + 1], LIMIT + 1.0,
                                          ALU.add, ALU.min).then_inc(u_used, 1)

                def multiply(m):
                    t = mem["t"][m % 2]
                    if mem["layer"] == 0:
                        dve.wait_ge(th_ready, m + 1)
                        chain(dve.scalar_tensor_tensor(mem["gc"][:, :], mem["th"][:, :], 1.0, mem["gc"][:, :],
                                                       ALU.add, ALU.mult))
                        dve.wait_ge(u_used, m + 1)
                        dve.scalar_tensor_tensor(t[:, :], t[:, :], 1.0 - LIMIT, mem["gc"][:, :],
                                                 ALU.max, ALU.mult).then_inc(a_ready, 1)
                    else:
                        dve.wait_ge(g_used, m + 1)
                        dve.tensor_tensor(t[:, :], (mem["gc"], mem["th"])[m % 2][:, :], up_bank[:, :],
                                          ALU.mult).then_inc(a_ready, 1)

                def down_low():
                    for q in range(2):
                        dve.wait_ge(dn_high, q + 1)
                        sl = slice(512 * q, 512 * (q + 1))
                        dve.tensor_tensor(mem["dnl"][:, sl], mem["raw"][:, sl], mem["dnh"][:, sl].bitcast(F32),
                                          ALU.subtract).then_inc(dn_split, 1)

                def add_down(c, half):
                    if c == 0 and half == 0:
                        dve.wait_ge(picked, 1)
                    dve.wait_ge(y_full, 2 * c + half + 1)
                    for i in range(2):
                        n = NT * c + 2 * half + i
                        ins = dve.scalar_tensor_tensor(acc[:, n, :], down_bank[:, D * i:D * (i + 1)],
                                                       mem["ce"][:, n:n + 1], acc[:, n, :], ALU.mult, ALU.add)
                    ins.then_inc(y_used, 1)

                if moe:
                    hidden(0)
                    down_low()
                    hidden(1)

                if kind == "mla":
                    flat = mem["sq"][:, :]
                    for t in range(NT):
                        dve.wait_ge(proj_ready, 2 * (t + 1))
                        dve.tensor_tensor(flat[:, 0:2 * D].rearrange("p (m o) -> p m o", m=2), qkr[:, t, 0:2, :],
                                          qkr[:, t, 0:2, :], ALU.mult).then_inc(dve_step, 1)
                        chain.n += 1
                        dve.wait_ge(dve_step, chain.n)
                        chain(dve.tensor_reduce(mem["qkn"][:, 2 * H * t:2 * H * (t + 1)],
                                                flat[:, 0:2 * D].rearrange("p (h o) -> p h o", o=HD), AX.X, ALU.add))
                    r = mem["qkn"][:, :].rearrange("p (t m h) -> p t m h", t=NT, m=2)
                    for m, by in ((0, 16.0), (1, 1.0)):
                        dve.tensor_scalar(r[:, :, m, :], r[:, :, m, :], by / HD, by * QK_EPS, ALU.mult,
                                          ALU.add).then_inc(qk_ms, 1)
                    clip(2)
                    dve.wait_ge(qk_std, 1)
                    chain(dve.reciprocal(mem["qkn"][:, :], mem["qkn"][:, :]))

                    def norm_heads(heads):
                        cols = slice(HD * heads.start, HD * heads.stop)
                        v = [qkr[:, :, m, cols].rearrange("p t (h o) -> p t h o", o=HD) for m in range(2)]
                        for m in range(2):
                            dve.tensor_tensor(v[m], v[m], bcast(r[:, :, m, heads], 3, HD), ALU.mult).then_inc(dve_step, 1)
                        chain.n += 2
                        dve.wait_ge(dve_step, chain.n)
                        for m in range(2):
                            w = bcast(bcast(mem["qkw"][:, m, :], 1, NT), 2, heads.stop - heads.start)
                            dve.tensor_tensor(v[m], v[m], w, ALU.mult).then_inc(dve_step, 1)
                        chain.n += 2
                        dve.wait_ge(dve_step, chain.n)
                        dve.tensor_tensor(qkr[:, :, 1, cols], qkr[:, :, 1, cols], qkr[:, :, 2, cols],
                                          ALU.add).then_inc(qk_ready, 1)

                    norm_heads(slice(0, 4))
                    multiply(2)
                    hidden(3)
                if kind == "gqa":
                    for n, t in enumerate(list(range(NT)) + [None]):
                        if n:
                            dve.wait_ge(qk_ready, 2 * n)
                        part, heads = (0, H) if t is not None else (1, HKV)
                        tiles = slice(t, t + 1) if t is not None else slice(0, NT)
                        dve.wait_ge(proj_ready, 2 * ((NT - 1 if t is None else t) + 1))
                        rows_qk = qkr[:, tiles, part, 0:HD * heads]
                        v = [rows_qk.rearrange("p t (h s o) -> p t h s o", s=2, o=HD // 2)[:, :, :, n, :] for n in range(2)]
                        size = NT * HD * HKV
                        tmp = [mem["sq"][:, size * n:size * n + (tiles.stop - tiles.start) * heads * HD // 2]
                               .rearrange("p (t h o) -> p t h o", h=heads, o=HD // 2) for n in range(2)]
                        cs, sn = (mem["cs"][:, tiles, n, :] for n in range(2))
                        dve.tensor_tensor(tmp[0], v[1], bcast(sn, 2, heads), ALU.mult).then_inc(dve_step, 1)
                        dve.tensor_tensor(tmp[1], v[0], bcast(sn, 2, heads), ALU.mult).then_inc(dve_step, 1)
                        chain.n += 2
                        dve.wait_ge(dve_step, chain.n)
                        flat_v = rows_qk.rearrange("p t (h o) -> p t h o", o=HD // 2)
                        chain(dve.tensor_tensor(flat_v, flat_v, bcast(cs, 2, 2 * heads), ALU.mult))
                        dve.tensor_tensor(v[0], v[0], tmp[0], ALU.subtract).then_inc(qk_ready, 1)
                        dve.tensor_tensor(v[1], v[1], tmp[1], ALU.add).then_inc(qk_ready, 1)
                if kind == "spm":
                    dve.wait_ge(x_act, 2 + 2 * NT)
                    dve.wait_ge(proj_ready, NT)
                    dve.tensor_scalar(small[:, 0:1], small[:, 0:1], 1.0, None, ALU.mult).then_inc(qk_ready, 1)
                if kind == "spm" and moe:
                    hidden(2)
                    hidden(3)

                def take_k(p):
                    dve.wait_ge(x_full, X.full(f"Tk{p}"))
                    dve.tensor_copy(mem["ksT"][p % 2][:, :], X.bank(f"Tk{p}")[:, :]).then_inc(x_dve, 1)

                def shift(p, between=None):
                    st, qs = mem["st"], mem["qst"][p % 2]
                    top = mem.get("top")
                    held = []
                    for u in range(NU):
                        if u == NU // 2 and between:
                            between()
                        bank = S.bank(("q", p, u))
                        dve.wait_ge(s_full, S.full(("q", p, u)))
                        for n, (j, t, first, width) in enumerate(Q_UNITS[u]):
                            last = n == len(Q_UNITS[u]) - 1
                            r = 2 * t + j
                            if kind == "spm":
                                ins = dve.max(top[:, 0, r, :], bank[:, first:first + width])
                            else:
                                ins = dve.reduce_max(st[:, 0, r:r + 1], bank[:, first:first + width], AX.X)
                            if last and not general:
                                ins.then_inc(s_dve, 1)
                            else:
                                ins.then_inc(dve_step, 1)
                                chain.n += 1
                            held.append((r, bank, first, width))
                    dve.wait_ge(dve_step, chain.n)
                    if not general:
                        dve.wait_ge(s_dve, S.uses[:S.full(("q", p, NU - 1))].count("dve"))
                    if kind != "spm":
                        chain(dve.tensor_scalar(st[:, 1, :], st[:, 0, :], -1.0, None, ALU.mult))
                    else:
                        z = top[:, 0, :, :]
                        dve.tensor_tensor(top[:, 1, :, :], z, z[:, :, 0:1].broadcast_to([P, 8, 8]), ALU.subtract).then_inc(dve_step, 1)
                        chain.n += 1
                        dve.wait_ge(dve_step, chain.n)
                        rel = top[:, 1, :, :].rearrange("p r k -> p (r k)")
                        chain(dve.tensor_tensor_scan(top[:, 2, :, :].rearrange("p r k -> p (r k)"),
                                                     mem["keep"][:, 0, :], rel, 0.0, ALU.mult, ALU.add))
                        chain(dve.tensor_tensor(top[:, 3, :, :].rearrange("p r k -> p (r k)"), rel,
                                                mem["keep"][:, 1, :], ALU.mult))
                        chain(dve.scalar_tensor_tensor(top[:, 4, :, :].rearrange("p r k -> p (r k)"),
                                                       top[:, 3, :, :].rearrange("p r k -> p (r k)"), 1.0,
                                                       top[:, 2, :, :].rearrange("p r k -> p (r k)"), ALU.add, ALU.is_gt))
                        chain(dve.tensor_reduce(st[:, 2, :], top[:, 4, :, :], AX.X, ALU.add))
                        chain(dve.tensor_tensor(top[:, 3, :, :], top[:, 1, :, :], top[:, 4, :, :], ALU.mult))
                        chain(dve.tensor_reduce(st[:, 3, :], top[:, 3, :, :], AX.X, ALU.add))
                        chain(dve.reciprocal(st[:, 4, :], st[:, 2, :]))
                        chain(dve.scalar_tensor_tensor(st[:, 5, :], st[:, 3, :], -1.0, st[:, 4, :], ALU.add, ALU.mult))
                        chain(dve.scalar_tensor_tensor(st[:, 1, :], st[:, 5, :], -1.0, z[:, :, 0], ALU.mult, ALU.subtract))
                        if not general:
                            chain(dve.tensor_tensor(flag[:, :], flag[:, :], top[:, 4, :, 7], ALU.max))
                        else:
                            newton(p, held, st)
                    rv = st[:, 1, :].rearrange("p (t j) -> p t j", j=2)
                    chain(dve.tensor_copy(qs[:, :, :, SHIFT].bitcast(F32R), rv))
                    dve.tensor_tensor(qs[:, :, :, SHIFT + 1], rv, qs[:, :, :, SHIFT], ALU.subtract).then_inc(shift_ready, 1)

                def newton(p, held, st):
                    with dve.Fori(0, NEWTON):
                        for r, bank, first, width in held:
                            region = bank[:, first:first + width]
                            junk = mem["junk"][:, 0:width]
                            dve.scalar_tensor_tensor(junk, region, st[:, 1, r:r + 1], mem["zero"][:, 0:width],
                                                     ALU.add, ALU.max, accum_out=st[:, 2, r:r + 1])
                            dve.drain()
                            dve.scalar_tensor_tensor(junk, region, st[:, 1, r:r + 1], mem["zero"][:, 0:width],
                                                     ALU.add, ALU.is_gt, accum_out=st[:, 3, r:r + 1])
                            dve.drain()
                        dve.reciprocal(st[:, 4, :], st[:, 3, :])
                        dve.drain()
                        dve.scalar_tensor_tensor(st[:, 5, :], st[:, 2, :], -1.0, st[:, 4, :], ALU.add, ALU.mult)
                        dve.drain()
                        dve.tensor_tensor(st[:, 1, :], st[:, 1, :], st[:, 5, :], ALU.subtract)
                        dve.drain()
                    for u in range(NU):
                        dve.tensor_copy(st[:, 6, u:u + 1], st[:, 1, u:u + 1]).then_inc(s_dve, 1)

                def heads_out(p):
                    dve.wait_ge(x_full, X.full(f"N{p}"))
                    o = X.bank(f"N{p}")[:, :].rearrange("p (t j s n) -> p t j s n", t=NT, j=2, s=2)
                    to = ctxt[:, :, 2 * HD * p:2 * HD * (p + 1)].rearrange("p t (j d) -> p t j d", j=2)
                    if kind == "spm":
                        dve.tensor_copy(to[:, 0, :, :], o[:, 0, :, 0, 0:HD]).then_inc(dve_step, 1)
                        chain.n += 1
                        dve.tensor_copy(to[:, 1:NT, :, :], o[:, 1:NT, :, 0, 0:HD]).then_inc(dve_step, 1)
                        chain.n += 1
                        dve.wait_ge(dve_step, chain.n)
                        dve.tensor_tensor(to[:, 1:NT, :, :], to[:, 1:NT, :, :], o[:, 1:NT, :, 1, 0:HD],
                                          ALU.add).then_inc(x_dve, 1)
                    else:
                        both = mem["both"]
                        chain(dve.tensor_copy(both[:, :, :, :], o[:, :, :, 0, 0:HD + 1]))
                        dve.tensor_tensor(both[:, 1:NT, :, :], both[:, 1:NT, :, :], o[:, 1:NT, :, 1, 0:HD + 1],
                                          ALU.add).then_inc(x_dve, 1)
                        dve.wait_ge(x_dve, X.uses[:X.full(f"N{p}")].count("dve"))
                        rec = mem["rec"][:, :].rearrange("p (t j) -> p t j", j=2)
                        chain(dve.reciprocal(rec, both[:, :, :, HD]))
                        chain(dve.tensor_tensor(to, both[:, :, :, 0:HD], bcast(rec, 3, HD), ALU.mult))

                if attn:
                    take_k(0)
                    shift(0)
                    if kind == "mla":
                        norm_heads(slice(4, H))
                    if not moe:
                        for p in range(NP + late):
                            if p + 1 < NP:
                                take_k(p + 1)
                                shift(p + 1)
                            if p >= 1:
                                heads_out(p - 1)
                    for p in range(NP if moe else 0):
                        c = p + 1
                        if p + 1 < NP:
                            take_k(p + 1)
                        if moe and c < NCH:
                            hidden(FC * c)
                        if moe:
                            add_down(c - 1, 0)
                        if moe and c < NCH:
                            hidden(FC * c + 1)
                        second = (lambda: add_down(c - 1, 1)) if moe else None
                        if p + 1 < NP:
                            shift(p + 1, second)
                        elif moe:
                            second()
                            split_low(mem, dve, gu_high, gu_split)
                        if moe and c < NCH:
                            hidden(FC * c + 2)
                        heads_out(p)
                        if moe and c < NCH:
                            hidden(FC * c + 3)
                    dve.wait_ge(x_dve, X.uses[:X.full(f"N{NP - 1}")].count("dve"))
                    if kind == "mla":
                        dve.wait_ge(y_used, 2 * NCH)
                        dve.tensor_tensor(acc[:, at, :], acc[:, at, :], ctxt, ALU.add).then_inc(ctx_ready, 1)
                    else:
                        dve.tensor_scalar(small[:, 1:2], small[:, 1:2], 1.0, None, ALU.mult).then_inc(ctx_ready, 1)
                        for n in range(2):
                            y = X.bank(f"Y{n}")[:, :].rearrange("p (t d) -> p t d", t=2)
                            dve.wait_ge(x_full, X.full(f"Y{n}"))
                            if kind == "spm":
                                dve.wait_ge(loaded, 16)
                                dve.tensor_tensor(qkr[:, 2 * n:2 * n + 2, 0, :], y, qkr[:, 2 * n:2 * n + 2, 1, :],
                                                  ALU.add).then_inc(h_ready, 1)
                            else:
                                dve.wait_ge(xn_ready, 2 * NT)
                                dve.tensor_tensor(ctxt[:, 2 * n:2 * n + 2, :], y, xb[:, 2 * n:2 * n + 2, :],
                                                  ALU.add).then_inc(x_dve, 1)
                                dve.wait_ge(x_dve, X.uses[:X.full(f"Y{n}")].count("dve"))
                                dve.tensor_scalar(ctxt[:, 2 * n:2 * n + 2, :], ctxt[:, 2 * n:2 * n + 2, :], 100.0, -100.0,
                                                  ALU.min, ALU.max).then_inc(h_ready, 1)
                if kind == "gqa":
                    dve.wait_ge(h_ready, 2)
                    dve.wait_ge(sq_ready, NT)
                    dve.tensor_scalar(small[:, 36:40], small[:, 32:36], 1.0 / D, RMS_EPS, ALU.mult,
                                      ALU.add).then_inc(hms_ready, 1)
                    dve.wait_ge(hstd_ready, 1)
                    for t in range(NT):
                        dve.tensor_scalar(xb[:, t, :], ctxt[:, t, :], small[:, 28 + t:29 + t], None,
                                          ALU.mult).then_inc(hn_ready, 1)
                if routed:
                    name = "Th" if kind == "gqa" else "Tx"
                    for c in range(DC):
                        dve.wait_ge(rest_hi, c + 1)
                        dve.wait_ge(xT_ready, c + 1)
                        dve.tensor_tensor(rest_l[:, c, at_tok], xT[:, c, :], rest_h[:, c, at_tok].bitcast(F32),
                                          ALU.subtract).then_inc(x_dve, 1)
                    dve.wait_ge(x_full, X.full("R"))
                    lg = rt[:, 0, :].rearrange("p (t e) -> p t e", e=E)
                    logits = X.bank("R")[:, 0:NT * E].rearrange("p (t e) -> p t e", e=E)
                    dve.tensor_tensor(lg, logits, bcast(mem["rb"][:, :], 1, NT), ALU.add).then_inc(x_dve, 1)
                    dve.wait_ge(x_dve, X.uses[:X.full("R")].count("dve"))
                    big = mem["big"]
                    cmp = [big[:, n, :].rearrange("p (t i j) -> p t i j", t=NT, i=E) for n in range(2)]
                    other, own = bcast(lg, 2, E), bcast(lg, 3, E)
                    dve.tensor_tensor(cmp[0], other, own, ALU.is_gt).then_inc(dve_step, 1)
                    chain.n += 1
                    chain(dve.tensor_tensor(cmp[1], other, own, ALU.is_equal))
                    chain(dve.tensor_tensor(big[:, 1, :].rearrange("p (t n) -> p t n", t=NT),
                                            big[:, 1, :].rearrange("p (t n) -> p t n", t=NT),
                                            bcast(tie[:, :, :].rearrange("p i j -> p (i j)"), 1, NT), ALU.mult))
                    chain(dve.tensor_tensor(big[:, 0, :], big[:, 0, :], big[:, 1, :], ALU.add))
                    chain(dve.tensor_reduce(rt[:, 1, :], big[:, 0, :].rearrange("p (n j) -> p n j", j=E), AX.X, ALU.add))
                    chain(dve.tensor_scalar(rt[:, 2, :], rt[:, 1, :], float(routed), None, ALU.is_lt))
                    chain(dve.reduce_max(rt[:, 3, 0:NT], lg, AX.X))
                    dve.tensor_tensor(rt[:, 4, :].rearrange("p (t e) -> p t e", e=E), lg, bcast(rt[:, 3, 0:NT], 2, E),
                                      ALU.subtract).then_inc(lg_ready, 1)
                    dve.wait_ge(exp_ready, 1)
                    chain(dve.tensor_tensor(rt[:, 5, :], rt[:, 5, :], rt[:, 2, :], ALU.mult))
                    chain(dve.reduce_sum(rt[:, 3, 8:8 + NT], rt[:, 5, :].rearrange("p (t e) -> p t e", e=E), AX.X))
                    chain(dve.reciprocal(rt[:, 3, 16:16 + NT], rt[:, 3, 8:8 + NT]))
                    dve.tensor_tensor(rt[:, 6, :].rearrange("p (t e) -> p t e", e=E),
                                      rt[:, 5, :].rearrange("p (t e) -> p t e", e=E),
                                      bcast(rt[:, 3, 16:16 + NT], 2, E), ALU.mult).then_inc(comb_ready, 1)
                    dve.wait_ge(comb_ready, 1)
                    dve.tensor_scalar(combine[:, at, :], rt[:, 6, :].rearrange("p (t e) -> p t e", e=E),
                                      0.5 if kind == "none" else 1.0, None, ALU.mult).then_inc(cc_ready, 1)
                    if kind == "none":
                        for n in range(2):
                            dve.wait_ge(x_full, X.full(f"B{n}"))
                            a = acc[:, bass.ds(it * NT + 2 * n, 2), :]
                            dve.tensor_tensor(a, a, X.bank(f"B{n}")[:, :].rearrange("p (t d) -> p t d", t=2),
                                              ALU.add).then_inc(x_dve, 1)

            @block.tensor
            def _(pe):
                def take(name):
                    former = X.before(name)
                    if former:
                        pe.wait_ge(x_rel[former[0]], former[1])
                    return X.bank(name)

                def up(m):
                    c, j = m // FC, m % FC
                    for bank, full, used, first in ((gate_bank, g_full, g_used, 0), (up_bank, u_full, mem["u_rel"](u_used, a_ready), F)):
                        if m >= 1:
                            pe.wait_ge(used, m)
                        terms = [(w, x, k) for w, x in ((mem["guh"], rest_h), (mem["guh"], rest_l), (mem["gul"], rest_h))
                                 for k in range(DC)]
                        for n, (w, x, k) in enumerate(terms):
                            col = 2 * F * k + first + P * j
                            mm = pe.matmul(bank[:, :], w[:, col:col + P], x[:, k, 512 * c:512 * (c + 1)],
                                           start=(n == 0), stop=(n == len(terms) - 1))
                        mm.then_inc(full, 1)

                def down(c, half):
                    pe.wait_ge(al_ready, FC * (c + 1))
                    if c == 0:
                        pe.wait_ge(dn_split, 2)
                    if c or half:
                        pe.wait_ge(y_used, 2 * c + half)
                    for i in range(2):
                        t = 2 * half + i
                        bank = down_bank[:, D * i:D * (i + 1)]
                        terms = [(a, w, j) for a, w in ((mem["ah"], mem["dnh"]), (mem["ah"], mem["dnl"]), (mem["al"], mem["dnh"]))
                                 for j in range(FC)]
                        for n, (a, w, j) in enumerate(terms):
                            mm = pe.matmul(bank, a[:, j, P * t:P * (t + 1)], w[:, D * j:D * (j + 1)],
                                           start=(n == 0), stop=(n == len(terms) - 1))
                    mm.then_inc(y_full, 1)

                def turn(name, blocks):
                    bank = take(name)
                    for n, b in enumerate(blocks):
                        mm = pe.transpose(bank[:, P * n:P * (n + 1)], b, ident[:, :])
                    mm.then_inc(x_full, 1)

                if moe:
                    up(0)
                pe.wait_ge(xn_ready, NT)
                rows_in = ctxt if kind == "gqa" else xb
                for c in range(DC):
                    turn(f"Tx{c}", [rows_in[:, t, P * c:P * (c + 1)] for t in range(NT)])
                if moe:
                    up(1)

                def scores(which, p, u):
                    name = (which, p, u)
                    former = S.before(name)
                    if former:
                        pe.wait_ge(s_rel[former[0]], former[1])
                    bank = S.bank(name)
                    unit = (Q_UNITS if which == "q" else K_UNITS)[u]
                    diag = min(first + (P * blk if which == "q" else 0) for _, blk, first, _ in unit)
                    pe.matmul(bank[:, diag:diag + P * len(unit)], ident_bf[:, :],
                              masks_bf[:, 0 if which == "q" else 1, 0:len(unit), :].rearrange("p n k -> p (n k)"),
                              start=True, stop=False, skip_group_check=True)
                    for n, (j, blk, first, width) in enumerate(unit):
                        last = n == len(unit) - 1
                        rows_q = slice(SW * j, SW * j + (SHIFT if which == "q" else SHIFT + 2))
                        if which == "q":
                            mm = pe.matmul(bank[:, first:first + width], mem["qsT"][rows_q, P * blk:P * (blk + 1)],
                                           mem["ksT"][p % 2][rows_q, 0:width], start=False, stop=last, skip_group_check=True)
                        else:
                            mm = pe.matmul(bank[:, first:first + width], mem["ksT"][p % 2][rows_q, P * blk:P * (blk + 1)],
                                           mem["qaT"][rows_q, T - width:T], start=False, stop=last, skip_group_check=True)
                    mm.then_inc(s_full, 1)

                def counts(ring, name, who):
                    return ring.uses[:ring.full(name)].count(who)

                if attn:
                    pe.wait_ge(x_act, counts(X, "Tx1", "act"))
                    for t in range(NT):
                        tok = slice(P * t, P * (t + 1))
                        w = mem["w"]
                        if kind == "mla":
                            for c, n in enumerate("ab"):
                                bank = take(f"proj{t}{n}")
                                pe.matmul(bank[:, :], xT[:, c, tok], w[:, :, :].rearrange("p m o -> p (m o)"),
                                          start=True, stop=True).then_inc(x_full, 1)
                        else:
                            n_a = 512 if kind == "spm" else 384
                            bank = take(f"proj{t}a")
                            for c in range(DC):
                                mm = pe.matmul(bank[:, 0:n_a], xT[:, c, tok], w[:, c, 0:n_a], start=(c == 0), stop=(c == 1))
                            mm.then_inc(x_full, 1)
                            if kind == "spm":
                                bank = take(f"proj{t}b")
                                for c in range(DC):
                                    mm = pe.matmul(bank[:, 0:D], xT[:, c, tok], w[:, c, 512:768], start=(c == 0), stop=(c == 1))
                                mm.then_inc(x_full, 1)
                    if moe:
                        up(2)
                        up(3)

                    def turn_q(name, p):
                        turn(name, [mem["qst"][p % 2][:, t, :, :].rearrange("p j n -> p (j n)") for t in range(NT)])

                    def turn_k(p):
                        turn(f"Tk{p}", [mem["kst"][:, t, :, :].rearrange("p j n -> p (j n)") for t in range(NT)])

                    pe.wait_ge(stack_ready, 1)
                    turn_q("Tq0", 0)
                    turn_k(0)
                    pe.wait_ge(x_act, counts(X, "Tq0", "act"))
                    pe.wait_ge(x_dve, counts(X, "Tk0", "dve"))
                    for u in range(NU):
                        scores("q", 0, u)
                    def outputs(p):
                        pe.wait_ge(s_act, counts(S, ("k", p, NU - 1), "act"))
                        bank = take(f"O{p}")
                        for kbs in ((0, 1), (3, 2)):
                            for j in range(2):
                                for half, kb in enumerate(kbs):
                                    h = 2 * p + j
                                    vh = h // (H // HKV) if kind == "gqa" else h
                                    q0 = 32 * (2 * j + half)
                                    mm = pe.matmul(bank[q0:q0 + HD + 1, P * kb:T], V[:, kb, vh, :],
                                                   mem["pt"][:, j, PT_AT[kb]:PT_AT[kb] + T - P * kb],
                                                   start=(kb < 2), stop=(kb >= 2), skip_group_check=True)
                        mm.then_inc(x_full, 1)

                    def outputs_by_rows(p):
                        pe.wait_ge(x_act, counts(X, f"O{p}", "act"))
                        turn(f"N{p}", [mem["oT"][:, P * t:P * (t + 1)] for t in range(NT)])

                    if not moe:
                        for p in range(NP + late):
                            if p + 1 < NP:
                                pe.wait_ge(stack_ready, p + 2)
                                turn_q(f"Tq{p + 1}", p + 1)
                                turn_k(p + 1)
                            if p < NP:
                                pe.wait_ge(shift_ready, p + 1)
                                turn_q(f"Ta{p}", p)
                            if p + 1 < NP:
                                pe.wait_ge(x_act, counts(X, f"Tq{p + 1}", "act"))
                                pe.wait_ge(x_dve, counts(X, f"Tk{p + 1}", "dve"))
                                for u in range(NU):
                                    scores("q", p + 1, u)
                            if p >= 1:
                                outputs(p - 1)
                            if p < NP:
                                pe.wait_ge(x_act, counts(X, f"Ta{p}", "act"))
                                for u in range(NU):
                                    scores("k", p, u)
                            if p >= 1:
                                outputs_by_rows(p - 1)
                    for p in range(NP if moe else 0):
                        c = p + 1
                        pe.wait_ge(shift_ready, p + 1)
                        turn_q(f"Ta{p}", p)
                        if p + 1 < NP:
                            pe.wait_ge(stack_ready, p + 2)
                            turn_q(f"Tq{p + 1}", p + 1)
                            turn_k(p + 1)
                        if c < NCH:
                            up(FC * c)
                        pe.wait_ge(x_act, counts(X, f"Ta{p}", "act"))
                        for u in range(NU // 2):
                            scores("k", p, u)
                        down(c - 1, 0)
                        for u in range(NU // 2, NU):
                            scores("k", p, u)
                        if c < NCH:
                            up(FC * c + 1)
                        if p + 1 < NP:
                            pe.wait_ge(x_act, counts(X, f"Tq{p + 1}", "act"))
                            pe.wait_ge(x_dve, counts(X, f"Tk{p + 1}", "dve"))
                            for u in range(NU // 2):
                                scores("q", p + 1, u)
                        down(c - 1, 1)
                        if p + 1 < NP:
                            for u in range(NU // 2, NU):
                                scores("q", p + 1, u)
                        outputs(p)
                        if c < NCH:
                            up(FC * c + 2)
                        outputs_by_rows(p)
                        if c < NCH:
                            up(FC * c + 3)
                    if kind != "mla":
                        pe.wait_ge(ctx_ready, 1)
                        for c in range(DC):
                            turn(f"Tc{c}", [ctxt[:, t, P * c:P * (c + 1)] for t in range(NT)])
                        pe.wait_ge(x_act, counts(X, "Tc1", "act"))
                        for n in range(2):
                            bank = take(f"Y{n}")
                            for i in range(2):
                                for c in range(DC):
                                    t = 2 * n + i
                                    mm = pe.matmul(bank[:, D * i:D * (i + 1)], xT[:, c, P * t:P * (t + 1)],
                                                   mem["wo"][:, c, :], start=(c == 0), stop=(c == 1))
                            mm.then_inc(x_full, 1)
                if kind == "gqa":
                    pe.wait_ge(hn_ready, NT)
                    for c in range(DC):
                        turn(f"Th{c}", [xb[:, t, P * c:P * (c + 1)] for t in range(NT)])
                if routed:
                    pe.wait_ge(xT_ready, DC)
                    bank = take("R")
                    for t in range(NT):
                        for c in range(DC):
                            mm = pe.matmul(bank[:, E * t:E * (t + 1)], xT[:, c, P * t:P * (t + 1)], mem["wr"][:, c, :],
                                           start=(c == 0), stop=(c == 1))
                    mm.then_inc(x_full, 1)
                if kind == "none":
                    pe.wait_ge(comb_ready, 1)
                    bank = take("Cc")
                    for t in range(NT):
                        mm = pe.transpose(bank[0:E, P * t:P * (t + 1)], rt[:, 6, E * t:E * (t + 1)], ident[:, :])
                    mm.then_inc(x_full, 1)
                    pe.wait_ge(x_act, counts(X, "Cc", "act"))
                    for n in range(2):
                        bank = take(f"B{n}")
                        for i in range(2):
                            t = 2 * n + i
                            mm = pe.matmul(bank[:, D * i:D * (i + 1)], mem["cT"][:, P * t:P * (t + 1)], mem["db"][:, :],
                                           start=True, stop=True)
                        mm.then_inc(x_full, 1)
        done()

    def load(pairs, fills=()):
        new, done = sem_maker()
        loaded, filled = new("loaded"), new("filled")
        with nc.Block() as block:
            @block.sync
            def _(sp):
                for to, frm in pairs:
                    sp.dma_start(to, frm).then_inc(loaded, 16)
                sp.wait_ge(loaded, 16 * len(pairs))

            @block.vector
            def _(dve):
                for to, value in fills:
                    dve.memset(to, value).then_inc(filled, 1)
                if fills:
                    dve.wait_ge(filled, len(fills))
        done()

    def first_rows(z_stored):
        with nc.Block() as block:
            @block.sync
            def _(sp):
                sp.dma_start(xb[:, :, :], x1_rows[0]).then_inc(z_stored, 16)
                sp.wait_ge(z_stored, 16)
        nc.all_engine_barrier()

    def attention_buffers(st, kind):
        mem = {
            "qst": [sb(f"qst{i}", [P, NT, 2, SW], F32, st) for i in range(2)],
            "kst": sb("kst", [P, NT, 2, SW], F32, st),
            "qsT": sb("qsT", [P, T], F32R, st),
            "ksT": [sb(f"ksT{i}", [P, T], F32R, st) for i in range(2)],
            "qaT": sb("qaT", [P, T], F32R, st),
            "pt": sb("pt", [P, 2, PT_W], F32, st),
            "oT": sb("oT", [P, T], F32, st),
            "st": sb("st", [P, 8, 8], F32, st),
            "rec": sb("rec", [P, 8], F32, st),
            "both": sb("both", [P, NT, 2, HD + 1], F32, st),
        }
        fills = [(mem["qst"][i][:, :, :, SHIFT:SW], 0.0) for i in range(2)] + [(mem["kst"][:, :, :, SHIFT:SW], 1.0)]
        pairs = []
        if kind == "spm":
            mem["top"] = sb("top", [P, 5, 8, 8], F32, st)
            mem["keep"] = sb("keep", [P, 2, 64], F32, st)
            pairs.append((mem["keep"][:, :, :], dram["c_keep"]))
        return mem, pairs, fills

    def expert_buffers(st, mem, layer):
        mem.update({
            "layer": layer,
            "raw": sb("raw", [P, DC * 2 * F], F32, st),
            "guh": sb("guh", [P, DC * 2 * F], F32R, st),
            "gul": sb("gul", [P, DC * 2 * F], F32R, st),
            "dnh": sb("dnh", [P, FC * D], F32R, st),
            "dnl": sb("dnl", [P, FC * D], F32R, st),
            "gc": sb("gc", [P, 512], F32, st),
            "th": sb("th", [P, 512], F32, st),
            "t": [sb(f"t{i}", [P, 512], F32, st) for i in range(2)],
            "ah": sb("ah", [P, FC, 512], F32R, st),
            "al": sb("al", [P, FC, 512], F32R, st),
            "ce": sb("ce", [P, B * NT], F32, st),
            "gu_dram": dram[f"gu{layer}"],
            "dn_dram": dram[f"dn{layer}"],
            "u_rel": (lambda u_used, a_ready: u_used) if layer == 0 else (lambda u_used, a_ready: a_ready),
        })
        return [(mem["raw"][:, :], mem["gu_dram"][E - 1])]

    setup()
    with ExitStack() as st:
        mem = {"wr": sb("wr", [P, DC, E], F32, st), "rb": sb("rb", [P, E], F32, st), "db": sb("db", [E, D], F32, st),
               "cT": sb("cT", [E, T], F32, st), "big": sb("big", [P, 2, NT * E * E], F32, st)}
        load([(mem["wr"][:, :, :], dram["wr0"]), (mem["rb"][:, :], dram["rb0"]), (mem["db"][:, :], dram["db0"])])
        with nc.Fori(0, B) as it:
            iteration(it, "none", False, mem)
    with ExitStack() as st:
        mem, pairs, fills = attention_buffers(st, "mla")
        mem["w"] = sb("w_mla", [P, 4, P], F32, st)
        mem["qkn"] = sb("qkn", [P, NT * 2 * H], F32, st)
        mem["qkw"] = sb("qkw", [P, 2, HD], F32, st)
        mem["biases"] = sb("biases", [P, E, 2 * FC], F32, st)
        mem["be"] = sb("be", [P, 2 * FC], F32, st)
        pairs += expert_buffers(st, mem, 0)
        mem["sq"] = mem["oT"]
        pairs += [(xb[:, :, :], x_rows[0]), (mem["qkw"][:, :, :], dram["qkw"]), (mem["biases"][:, :, :], dram["gub"])]
        fold(mem["w"])
        load(pairs, fills)
        new, done = sem_maker()
        one = new("one")
        with nc.Block() as block:
            @block.vector
            def _(dve):
                dve.tensor_scalar(mem["biases"][:, :, FC:2 * FC], mem["biases"][:, :, FC:2 * FC], 1.0, None,
                                  ALU.add).then_inc(one, 1)
                dve.wait_ge(one, 1)
        done()
        split_first(mem)
        with nc.Fori(0, B) as it:
            iteration(it, "mla", True, mem)
    with ExitStack() as st:
        mem, pairs, fills = attention_buffers(st, "gqa")
        mem.update({"w": sb("w_gqa", [P, DC, 384], F32, st), "wo": sb("wo_gqa", [P, DC, D], F32, st),
                    "ln": sb("ln", [P, 4], F32, st), "wr": sb("wr", [P, DC, E], F32, st), "rb": sb("rb", [P, E], F32, st),
                    "cs": sb("cs", [P, NT, 2, HD // 2], F32, st), "sq": sb("sq", [P, 512], F32, st),
                    "big": sb("big", [P, 2, NT * E * E], F32, st)})
        pairs += [(mem["w"][:, :, :], dram["w_gqa"]), (mem["wo"][:, :, :], dram["wo_gqa"]), (mem["ln"][:, :], dram["ln"]),
                  (mem["wr"][:, :, :], dram["wr1"]), (mem["cs"][:, :, :, :], dram["c_rope"])]
        pairs.append((x1_rows[B], acc[:, 0:NT, :]))
        fills.append((mem["rb"][:, :], 0.0))
        load(pairs, fills)
        with nc.Fori(0, B) as it:
            iteration(it, "gqa", False, mem)
    with ExitStack() as st:
        mem, pairs, fills = attention_buffers(st, "spm")
        mem.update({"w": sb("w_spm", [P, DC, 3 * D], F32, st), "wo": sb("wo_spm", [P, DC, D], F32, st)})
        pairs += [(mem["w"][:, :, :], dram["w_spm"]), (mem["wo"][:, :, :], dram["wo_spm"])]
        pairs += expert_buffers(st, mem, 1)
        load(pairs, fills)
        split_first(mem)
        z_stored = nc.alloc_semaphore("z_stored")
        first_rows(z_stored)
        with nc.Fori(0, B) as it:
            iteration(it, "spm", True, mem, z_stored=z_stored)
        with nc.Block() as block:
            @block.sync
            def _(sp):
                sp.wait_ge(z_stored, 16 * (B + 1))
        nc.clear_and_free_semaphores([z_stored])
        nc.all_engine_barrier()

    new, done = sem_maker()
    folded, reduced, turned = new("folded"), new("reduced"), new("turned")
    with nc.Block() as block:
        @block.gpsimd
        def _(pool):
            pool.partition_all_reduce(flag_all[:, :], flag[:, :], P, RMAX).then_inc(reduced, 1)

        @block.vector
        def _(dve):
            dve.wait_ge(reduced, 1)
            dve.reduce_max(flag[:, 0:1], flag_all[:, :], AX.X).then_inc(folded, 1)
            dve.wait_ge(folded, 1)
            dve.tensor_copy(flag_int[:, :], flag[:, 0:1]).then_inc(turned, 1)
            dve.wait_ge(turned, 1)
    done()
    found = nc.values_load(flag_int[0:1, 0:1], min_val=0, max_val=1)
    with nc.If(found > 0):
        nc.all_engine_barrier()
        with ExitStack() as st:
            mem, pairs, fills = attention_buffers(st, "spm")
            mem.update({"w": sb("w_gen", [P, DC, 3 * D], F32, st), "wo": sb("wo_gen", [P, DC, D], F32, st),
                        "junk": sb("junk", [P, 512], F32, st), "zero": sb("zero", [P, 512], F32, st)})
            pairs += [(mem["w"][:, :, :], dram["w_spm"]), (mem["wo"][:, :, :], dram["wo_spm"])]
            fills.append((mem["zero"][:, :], 0.0))
            load(pairs, fills)
            z_again = nc.alloc_semaphore("z_again")
            first_rows(z_again)
            with nc.Fori(0, B) as it:
                iteration(it, "spm", False, mem, general=True, z_stored=z_again)
            with nc.Block() as block:
                @block.sync
                def _(sp):
                    sp.wait_ge(z_again, 16 * (B + 1))
            nc.clear_and_free_semaphores([z_again])
        nc.all_engine_barrier()
    nc.end_ifs()

    new, done = sem_maker()
    stored, clipped, summed = new("stored"), new("clipped"), new("summed")
    loaded = [new(f"loaded{b}") for b in range(B)]
    with ExitStack() as st:
        z = sb("z", [P, B * NT, D], F32, st)
        with nc.Block() as block:
            @block.sync
            def _(sp):
                for b in range(B):
                    sp.dma_start(z[:, NT * b:NT * (b + 1), :], z_rows[b]).then_inc(loaded[b], 16)
                for b in range(B):
                    sp.wait_ge(summed, b + 1)
                    sp.dma_start(out_rows[b], z[:, NT * b:NT * (b + 1), :]).then_inc(stored, 16)
                sp.wait_ge(stored, 16 * B)

            @block.vector
            def _(dve):
                for b in range(B):
                    tiles = slice(NT * b, NT * (b + 1))
                    dve.tensor_scalar(acc[:, tiles, :], acc[:, tiles, :], 100.0, -100.0, ALU.min,
                                      ALU.max).then_inc(clipped, 1)
                    dve.wait_ge(clipped, b + 1)
                    dve.wait_ge(loaded[b], 16)
                    dve.tensor_tensor(z[:, tiles, :], z[:, tiles, :], acc[:, tiles, :], ALU.add).then_inc(summed, 1)
    done()


def kernel(**inputs):
    import concourse.bacc as bacc
    from concourse.bass_utils import run_bass_kernel_spmd

    a = {k: np.asarray(v) for k, v in inputs.items()}

    def chunks(w):
        return np.ascontiguousarray(w.reshape(-1, P, w.shape[-1]).transpose(1, 0, 2))

    def experts(w):
        return np.ascontiguousarray(w.reshape(E, -1, P, w.shape[-1]).transpose(0, 2, 1, 3).reshape(E, P, -1))

    def everywhere(v):
        return np.ascontiguousarray(np.broadcast_to(v, (P,) + v.shape))

    f4 = np.float32
    rows = np.arange(P)
    mask = np.where(rows[None, :] > rows[:, None], f4(MASKED), f4(0))
    freqs = np.arange(T, dtype=f4)[:, None] * (f4(1) / f4(10000.0) ** (np.arange(0, HD, 2, dtype=f4) / f4(HD)))
    rope = np.stack([np.cos(freqs), np.sin(freqs)], 1).astype(f4)
    data = {
        "x": np.concatenate([a["L0_attn_x"].reshape(NTOK, D), a["L0_attn_x"][0]]),
        "c_ident": np.eye(P, dtype=f4),
        "c_masks": np.stack([mask, mask.T], 1),
        "c_tie": everywhere(np.tril(np.ones((E, E), f4), -1)),
        "c_block": (rows[:, None] // HD == np.arange(8)[None, :]).astype(f4),
        "c_keep": everywhere(np.stack([np.tile(np.r_[f4(0), np.ones(7, f4)], 8), np.tile(np.arange(1, 9, dtype=f4), 8)])),
        "c_rope": np.ascontiguousarray(rope.reshape(NT, P, 2, HD // 2).transpose(1, 0, 2, 3)),
        "dq": np.tile(a["L0_attn_W_DQ"], (1, 8)),
        "uq": a["L0_attn_W_UQ"].T,
        "dkv": chunks(np.tile(a["L0_attn_W_DKV"], (1, 8))),
        "ukv": chunks(a["L0_attn_W_UKV"].T),
        "kr": np.tile(a["L0_attn_W_KR"], (1, 8)),
        "qr": a["L0_attn_W_QR"],
        "wo": a["L0_attn_W_O"].T,
        "qkw": everywhere(np.stack([a["L0_attn_q_norm_w"], a["L0_attn_k_norm_w"]])),
        "wr0": chunks(a["L0_ffn_router_weight"].T),
        "rb0": everywhere(a["L0_ffn_router_bias"]),
        "gub": a["L0_ffn_gate_up_proj_bias"].reshape(E, 2 * FC, P).transpose(2, 0, 1),
        "db0": a["L0_ffn_down_proj_bias"],
        "gu0": np.roll(experts(a["L0_ffn_gate_up_proj"].transpose(0, 2, 1)), -1, axis=0),
        "dn0": experts(a["L0_ffn_down_proj"].transpose(0, 2, 1)),
        "w_gqa": chunks(np.concatenate([a["L1_ffn_Wq"], a["L1_ffn_Wk"], a["L1_ffn_Wv"]], 1)),
        "wo_gqa": chunks(a["L1_ffn_Wo"]),
        "ln": np.concatenate([a["L1_ffn_ln1_w"].reshape(DC, P).T, a["L1_ffn_ln2_w"].reshape(DC, P).T], 1),
        "wr1": chunks(a["L1_ffn_Wr"]),
        "gu1": np.roll(experts(np.concatenate([a["L1_ffn_Wg"], a["L1_ffn_Wu"]], 2)), -1, axis=0),
        "dn1": experts(a["L1_ffn_Wd"]),
        "w_spm": chunks(np.concatenate([a["L1_attn_Wq"].T, a["L1_attn_Wk"].T, a["L1_attn_Wv"].T], 1)),
        "wo_spm": chunks(a["L1_attn_Wo"].T),
    }
    nc = bacc.Bacc("TRN2", target_bir_lowering=False, num_devices=1, dynamic_dma_scratch_size=1024)
    data = {f"in_{k}": np.ascontiguousarray(v) for k, v in data.items()}
    dram = {k[3:]: nc.dram_tensor(k, list(v.shape), mybir.dt.from_np(v.dtype), kind="ExternalInput").ap()
            for k, v in data.items()}
    outs = {"out": nc.dram_tensor("out", [NTOK, D], F32, kind="ExternalOutput").ap()}
    program(nc, dram, outs)
    r = run_bass_kernel_spmd(nc, [data], core_ids=[0])
    return r.results[0]["out"].reshape(B, T, D)
```
